# Optimizing a Trainium2 kernel written in Bass

```python
import numpy as np
import jax
import jax.numpy as jnp

def _softmax(x, axis=-1):
    return jax.nn.softmax(x, axis=axis)

def _gelu(x):
    return jax.nn.gelu(x, approximate=True)

def _silu(x):
    return jax.nn.silu(x)

def _sigmoid(x):
    return jax.nn.sigmoid(x)

def _layernorm(x, axis=-1, eps=1e-05):
    m = jnp.mean(x, axis=axis, keepdims=True)
    v = jnp.var(x, axis=axis, keepdims=True)
    return (x - m) / jnp.sqrt(v + eps)

def _scatter_add(tgt, idx, src, axis=0):
    return tgt.at[idx].add(src)

def _segment_sum(src, seg, n):
    return jax.ops.segment_sum(src, seg, n)
kernel_name = 'mk_cond_seq_d1_seqx_r4_6c8ee7'

def setup_inputs(seed: int=0):
    np.random.seed(seed)
    _w = jnp.asarray

    def _rec_inputs():
        import jax
        import jax.numpy as jnp
        _rk = jax.random.key(seed)
        x = 1.648e-05 + 1 * jax.random.normal(jax.random.fold_in(_rk, 1), (32, 256, 288), jnp.float32)
        _lenS = 256 - jax.random.randint(jax.random.fold_in(_rk, 7), (32,), 0, max(1, 256 // 4) + 1, jnp.int32)
        _lenS2 = 256 - jax.random.randint(jax.random.fold_in(_rk, 8), (32,), 0, max(1, 256 // 4) + 1, jnp.int32)
        cond_1152 = 0.00914911 + 1.00357 * jax.random.normal(jax.random.fold_in(_rk, 11), (32, 288), jnp.float32)
        return (x, cond_1152)
    x, cond_1152 = _rec_inputs()

    def _L0_cond_setup():
        import jax, jax.numpy as jnp
        import numpy as np
        B, L, C = (8, 256, 288)
        H = 16
        D = C // H
        FF = int(C * 4.0)
        EPS = 1e-06

        def _layernorm(x):
            mu = jnp.mean(x, axis=-1, keepdims=True)
            var = jnp.mean(jnp.square(x - mu), axis=-1, keepdims=True)
            return (x - mu) * jax.lax.rsqrt(var + EPS)

        def _modulate(x, shift, scale):
            return x * (1.0 + scale) + shift

        def _attention(h, W_qkv, b_qkv, W_proj, b_proj):
            b, l, c = h.shape
            qkv = h @ W_qkv + b_qkv
            qkv = qkv.reshape(b, l, 3, H, D)
            q, k, v = (qkv[:, :, 0], qkv[:, :, 1], qkv[:, :, 2])
            scale = D ** (-0.5)
            scores = jnp.einsum('blhd,bmhd->bhlm', q * scale, k)
            attn = jax.nn.softmax(scores, axis=-1)
            o = jnp.einsum('bhlm,bmhd->blhd', attn, v).reshape(b, l, c)
            return o @ W_proj + b_proj
        key = jax.random.key(seed)
        ks = jax.random.split(key, 12)
        s = 0.02
        return {'x': jax.random.normal(ks[0], (B, L, C), jnp.float32), 'c': jax.random.normal(ks[1], (B, 1, C), jnp.float32), 'W_qkv': jax.random.normal(ks[2], (C, 3 * C), jnp.float32) * s, 'b_qkv': jnp.zeros((3 * C,), jnp.float32), 'W_proj': jax.random.normal(ks[3], (C, C), jnp.float32) * s, 'b_proj': jnp.zeros((C,), jnp.float32), 'W_fc1': jax.random.normal(ks[4], (C, FF), jnp.float32) * s, 'b_fc1': jnp.zeros((FF,), jnp.float32), 'W_fc2': jax.random.normal(ks[5], (FF, C), jnp.float32) * s, 'b_fc2': jnp.zeros((C,), jnp.float32), 'W_ada': jax.random.normal(ks[6], (C, 6 * C), jnp.float32) * s, 'b_ada': jnp.zeros((6 * C,), jnp.float32)}
    _L0_cond_all = _L0_cond_setup()
    _L0_cond_in = {k: v for k, v in _L0_cond_all.items() if k in ('W_qkv', 'b_qkv', 'W_proj', 'b_proj', 'W_fc1', 'b_fc1', 'W_fc2', 'b_fc2', 'W_ada', 'b_ada')}
    del _L0_cond_all
    return {'x': x, 'cond_1152': cond_1152, 'L0_cond_W_qkv': _L0_cond_in['W_qkv'], 'L0_cond_b_qkv': _L0_cond_in['b_qkv'], 'L0_cond_W_proj': _L0_cond_in['W_proj'], 'L0_cond_b_proj': _L0_cond_in['b_proj'], 'L0_cond_W_fc1': _L0_cond_in['W_fc1'], 'L0_cond_b_fc1': _L0_cond_in['b_fc1'], 'L0_cond_W_fc2': _L0_cond_in['W_fc2'], 'L0_cond_b_fc2': _L0_cond_in['b_fc2'], 'L0_cond_W_ada': _L0_cond_in['W_ada'], 'L0_cond_b_ada': _L0_cond_in['b_ada']}

def reference(x, cond_1152, L0_cond_W_qkv, L0_cond_b_qkv, L0_cond_W_proj, L0_cond_b_proj, L0_cond_W_fc1, L0_cond_b_fc1, L0_cond_W_fc2, L0_cond_b_fc2, L0_cond_W_ada, L0_cond_b_ada):
    import jax
    import jax.numpy as jnp

    def _L0_cond_ref(x, c, W_qkv, b_qkv, W_proj, b_proj, W_fc1, b_fc1, W_fc2, b_fc2, W_ada, b_ada):
        import jax, jax.numpy as jnp
        import numpy as np
        B, L, C = (8, 256, 288)
        H = 16
        D = C // H
        FF = int(C * 4.0)
        EPS = 1e-06

        def _layernorm(x):
            mu = jnp.mean(x, axis=-1, keepdims=True)
            var = jnp.mean(jnp.square(x - mu), axis=-1, keepdims=True)
            return (x - mu) * jax.lax.rsqrt(var + EPS)

        def _modulate(x, shift, scale):
            return x * (1.0 + scale) + shift

        def _attention(h, W_qkv, b_qkv, W_proj, b_proj):
            b, l, c = h.shape
            qkv = h @ W_qkv + b_qkv
            qkv = qkv.reshape(b, l, 3, H, D)
            q, k, v = (qkv[:, :, 0], qkv[:, :, 1], qkv[:, :, 2])
            scale = D ** (-0.5)
            scores = jnp.einsum('blhd,bmhd->bhlm', q * scale, k)
            attn = jax.nn.softmax(scores, axis=-1)
            o = jnp.einsum('bhlm,bmhd->blhd', attn, v).reshape(b, l, c)
            return o @ W_proj + b_proj
        ada = jax.nn.silu(c) @ W_ada + b_ada
        shift_msa, scale_msa, gate_msa, shift_mlp, scale_mlp, gate_mlp = jnp.split(ada, 6, axis=-1)
        h = _modulate(_layernorm(x), shift_msa, scale_msa)
        x = x + gate_msa * _attention(h, W_qkv, b_qkv, W_proj, b_proj)
        h = _modulate(_layernorm(x), shift_mlp, scale_mlp)
        mlp = jax.nn.gelu(h @ W_fc1 + b_fc1, approximate=True) @ W_fc2 + b_fc2
        x = x + gate_mlp * mlp
        return x
    x = _L0_cond_ref(x, cond_1152[:, None, :], L0_cond_W_qkv, L0_cond_b_qkv, L0_cond_W_proj, L0_cond_b_proj, L0_cond_W_fc1, L0_cond_b_fc1, L0_cond_W_fc2, L0_cond_b_fc2, L0_cond_W_ada, L0_cond_b_ada)
    return x

_drawn_inputs = setup_inputs


def setup_inputs(seed=0):
    import zlib

    import numpy as np

    out = dict(_drawn_inputs(seed))
    spreads = {'L0_cond_b_qkv': (0.0, 0.8),
     'L0_cond_b_proj': (0.0, 0.36),
     'L0_cond_b_fc1': (0.0, 0.8),
     'L0_cond_b_fc2': (0.0, 0.362),
     'L0_cond_b_ada': (0.0, 0.397)}
    factors = {'L0_cond_W_qkv': 8.0, 'L0_cond_W_proj': 5.523}
    for name, (base, spread) in spreads.items():
        noise = np.random.default_rng([zlib.crc32(name.encode()), seed]).standard_normal(out[name].shape)
        drawn = base * np.exp(spread * noise) if base else spread * noise
        out[name] = jnp.asarray(drawn.astype(out[name].dtype))
    for name, factor in factors.items():
        out[name] = (out[name] * factor).astype(out[name].dtype)
    return out
```

```python
from contextlib import ExitStack

import concourse.bass as bass
from concourse import mybir
from concourse.alu_op_type import AluOpType as ALU

F32 = mybir.dt.float32
F32R = mybir.dt.float32r
ACT = mybir.ActivationFunctionType
AX = mybir.AxisListType

B, L, C = 32, 256, 288
H = 16
D = C // H
FF = 4 * C
EPS = 1e-6
P = 128
NT = L // P
REM = C - 2 * P
KR = 3 * REM
CX = C + 2 * REM
KRB = KR + 2
PAIRS = H // 2
QUADS = H // 4
HB = 64
KS = 3 * D
KSM = KS + 1
VB = 32
NF = FF // P
FU = (NF + 1) // 2
NV = 4
SCALE = float(D) ** -0.5

QKV_USES = 2 + 3 * NT
MLP_USES = 2 + NT + 2 + FU + NT
TURN_USES = PAIRS + 2 * QUADS
USE_PROJ, USE_LT, USE_FC1, USE_FC2 = 2, 2 + NT, 4 + NT, 4 + NT + FU

SCHEDULE = [
    ("ln1", 1, 0), ("t1", 0, 0), ("fc2", -2, 0), ("t2", -1, 7), ("s", 0, 0), ("st", -1, 7),
    ("t1", 0, 1), ("fc2", -2, 1), ("pv", -1, 3), ("xt", 1, 0), ("on", -1, 3), ("t2", 0, 0), ("s", 0, 1),
    ("xt", 1, 1), ("st", 0, 0),
    ("t1", 0, 2), ("ot", -1, 0), ("t2", 0, 1), ("s", 0, 2), ("qkv", 1, 0), ("ot", -1, 1), ("st", 0, 1), ("qkv", 1, 1),
    ("t1", 0, 3), ("proj", -1, 0), ("pv", 0, 0), ("proj", -1, 1), ("on", 0, 0), ("t2", 0, 2), ("s", 0, 3),
    ("st", 0, 2), ("ln2", -1, 0), ("qkv", 1, 2),
    ("t1", 0, 4), ("qkv", 1, 3), ("t2", 0, 3), ("s", 0, 4), ("st", 0, 3), ("qkv", 1, 4),
    ("t1", 0, 5), ("lt", -1, 0), ("pv", 0, 1), ("on", 0, 1), ("t2", 0, 4), ("s", 0, 5), ("lt", -1, 1), ("st", 0, 4),
    ("qkv", 1, 5),
    ("t1", 0, 6), ("fc1", -1, 0), ("fc1", -1, 1), ("t2", 0, 5), ("s", 0, 6), ("fc1", -1, 2), ("fc1", -1, 3),
    ("fc1", -1, 4), ("st", 0, 5),
    ("t1", 0, 7), ("pv", 0, 2), ("on", 0, 2), ("t2", 0, 6), ("s", 0, 7), ("st", 0, 6),
]


class Batch:

    def __init__(self, half, k):
        self.half, self.k = half, k
        self.par = k % 2

    def times(self, n, plus):
        return self.half * (2 * n) + (self.k * n + plus)

    def pairs(self, n, plus):
        return self.half * n + (self.k // 2 * n + plus)

    def number(self):
        return self.half * 2 + self.k


def wait(eng, sem, value):
    if not (isinstance(value, int) and value <= 0):
        eng.wait_ge(sem, value)


def run(eng, steps):
    def iteration(half, k, only=True):
        for name, off, n in SCHEDULE:
            if only and not 0 <= 2 * half + k + off < B:
                continue
            if name in steps:
                steps[name](Batch(half, k + off), n)

    for k in (-1, 0, 1):
        iteration(0, k)
    with eng.Fori(1, B // 2 - 1) as half:
        for k in (0, 1):
            iteration(half, k, only=False)
    for k in (B - 2, B - 1, B, B + 1):
        iteration(0, k)


def dit_block(nc, x, cond, w_qkv, b_qkv, w_proj, b_proj, w_fc1, b_fc1, w_fc2, b_fc2, w_ada, b_ada, out, gates_dram):
    with ExitStack() as ctx:
        def sb(name, shape, dt=F32):
            return ctx.enter_context(nc.sbuf_tensor(name, shape, dt))

        def sem(name):
            return ctx.enter_context(nc.semaphore(name))

        score_bank = [ctx.enter_context(nc.psum_tensor(f"score_bank{t}", [P, 512], F32)) for t in range(2)]
        st_bank = ctx.enter_context(nc.psum_tensor("st_bank", [P, 2, NT, L], F32))
        t1_bank = ctx.enter_context(nc.psum_tensor("t1_bank", [P, 512], F32))
        turn_bank = ctx.enter_context(nc.psum_tensor("turn_bank", [P, 512], F32))
        qkv_bank = ctx.enter_context(nc.psum_tensor("qkv_bank", [P, 512], F32))
        mlp_bank = ctx.enter_context(nc.psum_tensor("mlp_bank", [P, 512], F32))

        wq = sb("wq", [P, 5, 3 * C], F32R)
        wp = sb("wp", [P, 5, C], F32R)
        w1 = sb("w1", [P, 5, FF], F32R)
        w2 = sb("w2", [P, 2, NF, C], F32R)
        b2 = sb("b2", [2, C], F32R)
        ones_r = sb("ones_r", [2, P], F32R)
        ident = sb("ident", [P, P])
        ident_r = sb("ident_r", [P, P], F32R)
        minus_lo = sb("minus_lo", [P, 2])
        mhalf = sb("mhalf", [P, NT])
        ada_bias = sb("ada_bias", [P, NV * 3])
        mod = sb("mod", [P, NV * 3, B])
        xin = sb("xin", [P, 2, NT, C])
        xn = sb("xn", [P, NT, CX])
        mod1 = sb("mod1", [P, 6])
        stat1 = sb("stat1", [P, NT, 6])
        mv1 = sb("mv1", [P, NT, 2])
        ve1 = sb("ve1", [P, NT])
        rs1 = sb("rs1", [P, NT])
        v1 = sb("v1", [P, 3, L])
        xh1 = sb("xh1", [P, 2, L], F32R)
        xl1 = sb("xl1", [P, 2, L], F32R)
        xr1 = sb("xr1", [P, L], F32R)
        qs = sb("qs", [P, 2, NT, H, HB], F32R)
        ks = sb("ks", [P, 2, NT, H, HB], F32R)
        ve = sb("ve", [P, 2, NT, H, VB])
        qk1 = sb("qk1", [P, 2, 2, L], F32R)
        q2 = sb("q2", [P, 2, L], F32R)
        e = sb("e", [P, 4, 2, NT, L])
        ots = sb("ots", [P, L])
        rc = sb("rc", [P, NT, 4, 1])
        onat = sb("onat", [P, NT, CX])
        gate = sb("gate", [P, 2, 2, C])
        xres = sb("xres", [P, NT, C])
        tmp = sb("tmp", [P, NT, C])
        x1 = sb("x1", [P, NT, C])
        xn2 = sb("xn2", [P, NT, CX])
        mod2 = sb("mod2", [P, 6])
        stat2 = sb("stat2", [P, NT, 6])
        mv2 = sb("mv2", [P, NT, 2])
        ve2 = sb("ve2", [P, NT])
        rs2 = sb("rs2", [P, NT])
        v3 = sb("v3", [P, 3, L])
        xh3 = sb("xh3", [P, 2, L], F32R)
        xl3 = sb("xl3", [P, 2, L], F32R)
        xr3 = sb("xr3", [P, L], F32R)
        g = sb("g", [P, NF * L])
        gh = sb("gh", [P, NF * L], F32R)
        gl = sb("gl", [P, NF * L], F32R)

        zeroed = sem("zeroed")
        consts = sem("consts")
        iota_step = sem("iota_step")
        w_loaded = [sem(f"w_loaded{i}") for i in range(2)]
        w_hi = sem("w_hi")
        w_split = sem("w_split")
        ada_loaded = sem("ada_loaded")
        ada_exp = sem("ada_exp")
        silu_step = sem("silu_step")
        ada_turned = sem("ada_turned")
        ada_sT = sem("ada_sT")
        ada_mm = sem("ada_mm")
        mod_ready = sem("mod_ready")
        gates_stored = sem("gates_stored")
        x_loaded = [sem(f"x_loaded{i}") for i in range(2)]
        ln1_dve = sem("ln1_dve")
        rstd1 = sem("rstd1")
        mod1_set = sem("mod1_set")
        qkv_full = sem("qkv_full")
        qkv_drained = sem("qkv_drained")
        x1_hi = sem("x1_hi")
        x1_lo = sem("x1_lo")
        x1_rem = sem("x1_rem")
        qk_hi = sem("qk_hi")
        t1_full = sem("t1_full")
        t1_drained = sem("t1_drained")
        s_full = [sem(f"s_full{i}") for i in range(2)]
        s_max = [sem(f"s_max{i}") for i in range(2)]
        turn_full = sem("turn_full")
        turn_drained = sem("turn_drained")
        st_full = sem("st_full")
        e_ready = sem("e_ready")
        recip = sem("recip")
        gate_loaded = [sem(f"gate_loaded{i}") for i in range(2)]
        res_loaded = sem("res_loaded")
        mlp_full = sem("mlp_full")
        mlp_drained = sem("mlp_drained")
        o_ready = sem("o_ready")
        o_hi = sem("o_hi")
        summed = sem("summed")
        ln2_dve = sem("ln2_dve")
        rstd2 = sem("rstd2")
        mod2_set = sem("mod2_set")
        x3_hi = sem("x3_hi")
        x3_lo = sem("x3_lo")
        x3_rem = sem("x3_rem")
        g_hi = sem("g_hi")
        g_lo = sem("g_lo")
        stored = sem("stored")
        passed = sem("passed")

        stage = [g[:, 0:FF], g[:, FF:2 * FF]]
        loads = []
        for w, bias, dst, n in ((w_qkv, b_qkv, wq, 3 * C), (w_proj, b_proj, wp, C), (w_fc1, b_fc1, w1, FF)):
            loads += [("full", w, bias, dst, n, 0), ("full", w, bias, dst, n, 1), ("rem", w, bias, dst, n, 0)]
        loads += [("fc2", w_fc2, None, w2, 3 * C, f) for f in range(0, NF, 3)]
        loads.append(("b2", b_fc2, None, b2, C, 0))
        staged, load_count = [0, 0], []
        for i, load in enumerate(loads):
            staged[i % 2] += 16 * {"full": 1, "rem": 5, "fc2": 1, "b2": 2}[load[0]]
            load_count.append(staged[i % 2])

        K_ROWS = [(0, P), (P, P), (2 * P, REM)]
        e_flat = e[:, :, :, :, :].rearrange("p a b c d -> p (a b c d)")
        w_ada_sb = [e_flat[:, 0:6 * C], e_flat[:, 6 * C:12 * C],
                    ve[:, :, :, :, :].rearrange("p a b c d -> p (a b c d)")[0:REM, 0:6 * C]]
        c_in, c_exp = x1[0:B, 0, :], x1[0:B, 1, :]
        c_sig, c_silu = xn2[0:B, 0, 0:C], xn2[0:B, 1, 0:C]
        sT = onat[:, 0, 0:3 * B].rearrange("p (k b) -> p k b", k=3)
        gate_bias, gate_val = xres[0:B, :, :], gate[0:B, 1, :, :]
        MOD_OF = [0, 1, 3, 4]
        GATE_OF = [2, 5]
        MOD_PS = score_bank[0][:, 0:NV * 3 * B].rearrange("p (v b) -> p v b", b=B)
        N_ADA = 4 + NV * 5 + 2

        def products(xh, xl, xr, w):
            return [(xh[:, 0, :], w[:, 0, :]), (xh[:, 1, :], w[:, 1, :]), (xh[:, 0, :], w[:, 2, :]),
                    (xh[:, 1, :], w[:, 3, :]), (xl[:, 0, :], w[:, 0, :]), (xl[:, 1, :], w[:, 1, :]),
                    (xr[0:KRB, :], w[0:KRB, 4, :])]

        def turn_use(kind, n):
            return 4 * (n // 2) + n % 2 if kind == "t2" else 4 * n + (2 if kind == "pv" else 3)

        block = ctx.enter_context(nc.Block())

        @block.sync
        def _(sp):
            sp.dma_start(c_in, cond).then_inc(ada_loaded, 16)
            for k, (r0, nr) in enumerate(K_ROWS):
                sp.dma_start(w_ada_sb[k], w_ada[r0:r0 + nr, :]).then_inc(ada_loaded, 16)
            sp.wait_ge(zeroed, 1)
            b_col = b_ada.rearrange("(v c o) -> v c o", v=6, o=1)
            for i, v in enumerate(MOD_OF):
                for tile in range(2):
                    sp.dma_start(ada_bias[:, 3 * i + tile:3 * i + tile + 1],
                                 b_col[v, tile * P:(tile + 1) * P]).then_inc(ada_loaded, 16)
                for r in range(3):
                    sp.dma_start(ada_bias[REM * r:REM * (r + 1), 3 * i + 2:3 * i + 3],
                                 b_col[v, 2 * P:C]).then_inc(ada_loaded, 16)
            for i, v in enumerate(GATE_OF):
                sp.dma_start(gate_bias[:, i, :],
                             b_ada[v * C:(v + 1) * C].rearrange("(a c) -> a c", a=1).broadcast_to([B, C])
                             ).then_inc(ada_loaded, 16)

            for i, (kind, w, bias, dst, n, k) in enumerate(loads):
                if i >= 2:
                    sp.wait_ge(w_split, i - 1)
                s, to = w_loaded[i % 2], stage[i % 2]
                if kind == "full":
                    sp.dma_start(to[:, 0:n], w[k * P:(k + 1) * P, :]).then_inc(s, 16)
                elif kind == "rem":
                    for r in range(3):
                        sp.dma_start(to[REM * r:REM * (r + 1), 0:n], w[2 * P:C, :]).then_inc(s, 16)
                    for r in range(2):
                        sp.dma_start(to[KR + r:KR + r + 1, 0:n], bias.rearrange("(a n) -> a n", a=1)).then_inc(s, 16)
                elif kind == "fc2":
                    sp.dma_start(to[:, 0:n].rearrange("p (f c) -> p f c", f=3),
                                 w[k * P:(k + 3) * P, :].rearrange("(f p) c -> p f c", p=P)).then_inc(s, 16)
                else:
                    for r in range(2):
                        sp.dma_start(to[r:r + 1, 0:n], w.rearrange("(a n) -> a n", a=1)).then_inc(s, 16)

            sp.wait_ge(mod_ready, 3)
            sp.dma_start(gates_dram, gate_val).then_inc(gates_stored, 16)
            sp.wait_ge(gates_stored, 16)

            def row(ap, b):
                return ap[b.k] if isinstance(b.half, int) and b.half == 0 else ap[b.number()]

            def load_x(b, _):
                wait(sp, ln1_dve, b.times(4, -4))
                sp.dma_start(xin[:, b.par], row(x, b).rearrange("(p t) c -> p t c", t=NT)
                             ).then_inc(x_loaded[b.par], 16)

            def load_residual(b, n):
                if n:
                    return
                wait(sp, summed, b.times(4, -2))
                sp.dma_start(xres[:, :, :], row(x, b).rearrange("(p t) c -> p t c", t=NT)
                             ).then_inc(res_loaded, 16)
                wait(sp, summed, b.times(4, -4))
                sp.dma_start(gate[:, b.par], row(gates_dram, b).unsqueeze(0).broadcast_to([P, 2, C])
                             ).then_inc(gate_loaded[b.par], 16)

            def store(b, n):
                if n == NT - 1:
                    sp.wait_ge(summed, b.times(4, 4))
                    sp.dma_start(row(out, b).rearrange("(p t) c -> p t c", t=NT), x1[:, :, :]).then_inc(stored, 16)

            run(sp, {"ln1": load_x, "ot": load_residual, "fc2": store})
            sp.wait_ge(stored, 16 * B)

        @block.tensor
        def _(pe):
            pe.wait_ge(consts, 2)
            pe.wait_ge(silu_step, 3)
            for k, (r0, nr) in enumerate(K_ROWS):
                last = nc.tensor.transpose(t1_bank[0:nr, k * B:(k + 1) * B], c_silu[:, r0:r0 + nr], ident[0:B, 0:B])
            last.then_inc(ada_turned, 1)
            pe.wait_ge(ada_sT, 1)
            pe.wait_ge(ada_loaded, 16 * N_ADA)
            for i, v in enumerate(MOD_OF):
                for tile, row, width in ((0, 0, P), (1, 0, P), (2, 0, REM), (2, REM, REM), (2, 2 * REM, REM)):
                    c0 = v * C + tile * P
                    for k, (_r, nr) in enumerate(K_ROWS):
                        last = nc.tensor.matmul(MOD_PS[row:row + width, 3 * i + tile, :],
                                                w_ada_sb[k][:, c0:c0 + width], sT[0:nr, k, :],
                                                start=(k == 0), stop=(k == 2))
            last.then_inc(ada_mm, 1)
            for i, v in enumerate(GATE_OF):
                for k, (_r, nr) in enumerate(K_ROWS):
                    last = nc.tensor.matmul([qkv_bank, mlp_bank][i][0:B, 0:C], sT[0:nr, k, :],
                                            w_ada_sb[k][:, v * C:(v + 1) * C], start=(k == 0), stop=(k == 2))
            last.then_inc(ada_mm, 1)
            pe.wait_ge(mod_ready, 3)
            pe.wait_ge(w_split, len(loads))

            def turn_x(bank, xn_, n):
                for t in range(NT):
                    if n == 0:
                        for c in range(2):
                            last = nc.tensor.transpose(bank[:, c * L + t * P:c * L + (t + 1) * P],
                                                       xn_[:, t, c * P:(c + 1) * P], ident[:, :])
                    else:
                        last = nc.tensor.transpose(bank[0:KR, t * P:(t + 1) * P], xn_[:, t, 2 * P:CX],
                                                   ident[:, :])
                return last

            def xt(b, n):
                pe.wait_ge(ln1_dve, b.times(4, 4))
                wait(pe, qkv_drained, b.times(QKV_USES, n))
                turn_x(qkv_bank, xn, n).then_inc(qkv_full, 1)

            def qkv(b, n):
                t, w = divmod(n, 3)
                pe.wait_ge(x1_lo, b.times(1, 1))
                pe.wait_ge(x1_rem, b.times(1, 1))
                pe.wait_ge(qkv_drained, b.times(QKV_USES, 2 + n))
                pr = products(xh1, xl1, xr1, wq)
                for i, (xa, wa) in enumerate(pr):
                    last = nc.tensor.matmul(qkv_bank[:, 0:C], xa[:, t * P:(t + 1) * P], wa[:, w * C:(w + 1) * C],
                                            start=(i == 0), stop=(i == len(pr) - 1))
                last.then_inc(qkv_full, 1)

            def t1(b, j):
                if j == 0:
                    pe.wait_ge(qkv_drained, b.times(QKV_USES, QKV_USES))
                wait(pe, t1_drained, b.times(PAIRS, j))
                for i, src in enumerate((qs, ks)):
                    for t in range(NT):
                        last = nc.tensor.transpose(t1_bank[:, i * L + t * P:i * L + (t + 1) * P].bitcast(F32R),
                                                   src[:, b.par, t, 2 * j:2 * j + 2, :], ident_r[:, :])
                last.then_inc(t1_full, 1)

            def s(b, j):
                pe.wait_ge(t1_drained, b.times(PAIRS, j + 1))
                for i in range(2):
                    wait(pe, s_max[i], b.times(PAIRS, j))
                    rows = slice(HB * i, HB * i + KS)
                    for t in range(NT):
                        last = nc.tensor.matmul(score_bank[i][:, t * L:(t + 1) * L],
                                                qk1[rows, j % 2, 0, t * P:(t + 1) * P], qk1[rows, j % 2, 1, :],
                                                start=True, stop=True)
                    last.then_inc(s_full[i], 1)

            def t2(b, j):
                for i in range(2):
                    pe.wait_ge(s_max[i], b.times(PAIRS, j + 1))
                wait(pe, turn_drained, b.times(TURN_USES, turn_use("t2", j)))
                for t in range(NT):
                    last = nc.tensor.transpose(turn_bank[:, t * P:(t + 1) * P].bitcast(F32R),
                                               qs[:, b.par, t, 2 * j:2 * j + 2, :], ident_r[:, :])
                last.then_inc(turn_full, 1)

            def st(b, j):
                pe.wait_ge(turn_drained, b.times(TURN_USES, turn_use("t2", j) + 1))
                wait(pe, e_ready, b.times(PAIRS, j))
                for i in range(2):
                    rows = slice(HB * i, HB * i + KSM)
                    for u in range(NT):
                        last = nc.tensor.matmul(st_bank[:, i, u, :], qk1[rows, j % 2, 1, u * P:(u + 1) * P],
                                                q2[rows, j % 2, :], start=True, stop=True)
                last.then_inc(st_full, 1)

            def pv(b, q):
                pe.wait_ge(e_ready, b.times(PAIRS, 2 * q + 2))
                pe.wait_ge(turn_drained, b.times(TURN_USES, turn_use("pv", q)))
                for u in range(NT):
                    for c in range(4):
                        last = nc.tensor.matmul(turn_bank[VB * c:VB * (c + 1), 0:L], ve[:, b.par, u, 4 * q + c, :],
                                                e[:, 2 * (q % 2) + c // 2, c % 2, u, :],
                                                start=(u == 0), stop=(u == NT - 1))
                last.then_inc(turn_full, 1)

            def on(b, q):
                pe.wait_ge(turn_drained, b.times(TURN_USES, turn_use("on", q)))
                for t in range(NT):
                    last = nc.tensor.transpose(turn_bank[:, t * P:(t + 1) * P], ots[:, t * P:(t + 1) * P], ident[:, :])
                last.then_inc(turn_full, 1)

            def ot(b, n):
                pe.wait_ge(o_ready, b.times(1, 1))
                wait(pe, mlp_drained, b.times(MLP_USES, n))
                turn_x(mlp_bank, onat, n).then_inc(mlp_full, 1)

            def proj(b, t):
                pe.wait_ge(mlp_drained, b.times(MLP_USES, USE_PROJ + t))
                pr = products(xh3, xl3, xr3, wp)
                for i, (xa, wa) in enumerate(pr):
                    last = nc.tensor.matmul(mlp_bank[:, 0:C], xa[:, t * P:(t + 1) * P], wa,
                                            start=(i == 0), stop=(i == len(pr) - 1))
                last.then_inc(mlp_full, 1)

            def lt(b, n):
                pe.wait_ge(ln2_dve, b.times(4, 4))
                pe.wait_ge(mlp_drained, b.times(MLP_USES, USE_LT + n))
                turn_x(mlp_bank, xn2, n).then_inc(mlp_full, 1)

            def fc1(b, n):
                pe.wait_ge(x3_lo, b.times(1, 1))
                pe.wait_ge(x3_rem, b.times(1, 1))
                pe.wait_ge(mlp_drained, b.times(MLP_USES, USE_FC1 + n))
                for f in range(2 * n, min(2 * n + 2, NF)):
                    pr = products(xh3, xl3, xr3, w1)
                    for i, (xa, wa) in enumerate(pr):
                        last = nc.tensor.matmul(mlp_bank[:, (f % 2) * L:(f % 2 + 1) * L], wa[:, f * P:(f + 1) * P], xa,
                                                start=(i == 0), stop=(i == len(pr) - 1))
                last.then_inc(mlp_full, 1)

            def fc2(b, t):
                pe.wait_ge(g_lo, b.times(FU, FU))
                pe.wait_ge(mlp_drained, b.times(MLP_USES, USE_FC2 + t))
                nc.tensor.matmul(mlp_bank[:, 0:C], ones_r[:, :], b2[:, :], start=True, stop=False)
                for f in range(NF):
                    cols = slice(f * L + t * P, f * L + (t + 1) * P)
                    nc.tensor.matmul(mlp_bank[:, 0:C], gh[:, cols], w2[:, 0, f, :], start=False, stop=False)
                    nc.tensor.matmul(mlp_bank[:, 0:C], gh[:, cols], w2[:, 1, f, :], start=False, stop=False)
                    last = nc.tensor.matmul(mlp_bank[:, 0:C], gl[:, cols], w2[:, 0, f, :], start=False,
                                            stop=(f == NF - 1))
                last.then_inc(mlp_full, 1)

            run(pe, {"xt": xt, "qkv": qkv, "t1": t1, "s": s, "t2": t2, "st": st, "pv": pv, "on": on, "ot": ot,
                     "proj": proj, "lt": lt, "fc1": fc1, "fc2": fc2})

        @block.scalar
        def _(act):
            act.wait_ge(ada_loaded, 16 * N_ADA)
            nc.scalar.activation(c_exp, c_in, ACT.Exp, scale=-1.0).then_inc(ada_exp, 1)
            act.wait_ge(mod_ready, 3)

            def xt(b, n):
                pe_use = b.times(QKV_USES, n + 1)
                act.wait_ge(mod1_set, b.times(1, 1))
                if n == 0:
                    wait(act, x1_lo, b.times(1, 0))
                    wait(act, x1_rem, b.times(1, 0))
                act.wait_ge(qkv_full, pe_use)
                for c in (0, 1) if n == 0 else (2,):
                    rows = P if c < 2 else KR
                    last = nc.scalar.activation(v1[0:rows, c, :], qkv_bank[0:rows, (c % 2) * L:(c % 2 + 1) * L],
                                                ACT.Identity, bias=mod1[0:rows, c:c + 1], scale=mod1[0:rows, 3 + c:4 + c])
                last.then_inc(qkv_drained, 1)

            def qkv(b, n):
                t, w = divmod(n, 3)
                act.wait_ge(qkv_full, b.times(QKV_USES, 3 + n))
                src = qkv_bank[:, 0:C].rearrange("p (h d) -> p h d", h=H)
                if w == 2:
                    nc.scalar.copy(ve[:, b.par, t, :, 0:D], src).then_inc(qkv_drained, 1)
                else:
                    to = (qs[:, b.par, t, :, 0:2 * D], ks[:, b.par, t, :, D:KS])[w]
                    nc.scalar.copy(to.rearrange("p h (r d) -> p h r d", r=2),
                                   src.unsqueeze(2).broadcast_to([P, H, 2, D])).then_inc(qk_hi, 1)

            def t1(b, j):
                act.wait_ge(t1_full, b.times(PAIRS, j + 1))
                nc.scalar.copy(qk1[:, j % 2, :, :].rearrange("p i l -> p (i l)"), t1_bank[:, :]).then_inc(t1_drained, 1)

            def st(b, j):
                act.wait_ge(st_full, b.times(PAIRS, j + 1))
                nc.scalar.activation(e[:, j % 4, :, :, :].rearrange("p i u l -> p (i u l)"),
                                     st_bank[:, :, :, :].rearrange("p i u l -> p (i u l)"),
                                     ACT.Exp, scale=SCALE).then_inc(e_ready, 1)

            def pv(b, q):
                act.wait_ge(turn_full, b.times(TURN_USES, turn_use("pv", q) + 1))
                nc.scalar.copy(ots[:, :], turn_bank[:, 0:L]).then_inc(turn_drained, 1)

            def ot(b, n):
                act.wait_ge(mlp_full, b.times(MLP_USES, n + 1))
                if n == 0:
                    nc.scalar.copy(xh3[:, :, :].rearrange("p c l -> p (c l)"), mlp_bank[:, :]).then_inc(o_hi, 1)
                else:
                    nc.scalar.copy(xr3[0:KR, :], mlp_bank[0:KR, 0:L]).then_inc(o_hi, 1)

            def lt(b, n):
                act.wait_ge(mod2_set, b.times(1, 1))
                if n == 0:
                    wait(act, x3_lo, b.times(1, 0))
                    wait(act, x3_rem, b.times(1, 0))
                act.wait_ge(mlp_full, b.times(MLP_USES, USE_LT + n + 1))
                for c in (0, 1) if n == 0 else (2,):
                    rows = P if c < 2 else KR
                    last = nc.scalar.activation(v3[0:rows, c, :], mlp_bank[0:rows, (c % 2) * L:(c % 2 + 1) * L],
                                                ACT.Identity, bias=mod2[0:rows, c:c + 1], scale=mod2[0:rows, 3 + c:4 + c])
                last.then_inc(mlp_drained, 1)

            def fc1(b, n):
                wait(act, g_lo, b.times(FU, n + 1 - FU))
                act.wait_ge(mlp_full, b.times(MLP_USES, USE_FC1 + n + 1))
                cols = min(2 * L, NF * L - 2 * L * n)
                nc.scalar.activation(g[:, 2 * L * n:2 * L * n + cols], mlp_bank[:, 0:cols], ACT.Gelu_apprx_tanh
                                     ).then_inc(mlp_drained, 1)

            run(act, {"xt": xt, "qkv": qkv, "t1": t1, "st": st, "pv": pv, "ot": ot, "lt": lt, "fc1": fc1})

        @block.vector
        def _(dve):
            nc.vector.memset(ada_bias[:, :], 0.0).then_inc(zeroed, 1)
            nc.vector.memset(mod[:, :, :], 0.0)
            nc.vector.memset(minus_lo[:, :], 0.0).then_inc(w_hi, 1)
            dve.wait_ge(w_hi, 1)
            nc.vector.memset(minus_lo[REM:2 * REM, 0:1], -1.0)
            nc.vector.memset(minus_lo[KR:P, 0:1], -1.0)
            nc.vector.memset(minus_lo[0:REM, 1:2], -1.0).then_inc(w_hi, 1)
            dve.wait_ge(w_hi, 2)
            nc.vector.memset(minus_lo[KR:KR + 1, 0:1], 0.0)
            nc.vector.memset(minus_lo[0:1, 1:2], 0.0)
            nc.vector.memset(mhalf[:, :], -0.5)
            nc.vector.memset(ones_r[:, :].bitcast(F32), 1.0)
            nc.vector.memset(xr1[KR:KRB, :].bitcast(F32), 1.0)
            nc.vector.memset(xr3[KR:KRB, :].bitcast(F32), 1.0)
            dve.wait_ge(iota_step, 2)
            nc.vector.tensor_copy(ident_r[:, :], ident[:, :])
            nc.vector.memset(ks[:, :, :, :, KSM:HB].bitcast(F32), 0.0)
            nc.vector.memset(ks[:, :, :, :, KS:KSM].bitcast(F32), -1.0).then_inc(consts, 1)
            dve.wait_ge(ada_exp, 1)
            nc.vector.tensor_scalar(c_exp, c_exp, 1.0, None, ALU.add).then_inc(silu_step, 1)
            dve.wait_ge(silu_step, 1)
            nc.vector.reciprocal(c_sig, c_exp).then_inc(silu_step, 1)
            dve.wait_ge(silu_step, 2)
            nc.vector.tensor_tensor(c_silu, c_in, c_sig, ALU.mult).then_inc(silu_step, 1)
            for i in (1, 3):
                last = nc.vector.tensor_scalar(ada_bias[:, 3 * i:3 * i + 3], ada_bias[:, 3 * i:3 * i + 3], 1.0, None,
                                               ALU.add)
            last.then_inc(silu_step, 1)
            dve.wait_ge(ada_turned, 1)
            nc.vector.tensor_copy(sT[:, 0:2, :], t1_bank[:, 0:2 * B].rearrange("p (k b) -> p k b", k=2))
            nc.vector.tensor_copy(sT[0:REM, 2, :], t1_bank[0:REM, 2 * B:3 * B]).then_inc(ada_sT, 1)
            dve.wait_ge(ada_mm, 1)
            dve.wait_ge(silu_step, 4)
            bias4 = ada_bias[:, :].rearrange("p (v c) -> p v c", c=3)
            mod4 = mod[:, :, :].rearrange("p (v c) b -> p v c b", c=3)
            ps4 = MOD_PS.rearrange("p (v c) b -> p v c b", c=3)
            nc.vector.tensor_tensor(mod4[:, :, 0:2, :], ps4[:, :, 0:2, :],
                                    bias4[:, :, 0:2].unsqueeze(3).broadcast_to([P, NV, 2, B]), ALU.add
                                    ).then_inc(mod_ready, 1)
            nc.vector.tensor_tensor(mod4[0:KR, :, 2, :], ps4[0:KR, :, 2, :],
                                    bias4[0:KR, :, 2:3].broadcast_to([KR, NV, B]), ALU.add).then_inc(mod_ready, 1)
            dve.wait_ge(ada_mm, 2)
            nc.vector.tensor_tensor(gate_val[:, 0, :], qkv_bank[0:B, 0:C], gate_bias[:, 0, :], ALU.add)
            nc.vector.tensor_tensor(gate_val[:, 1, :], mlp_bank[0:B, 0:C], gate_bias[:, 1, :], ALU.add
                                    ).then_inc(mod_ready, 1)
            nc.vector.memset(ve[:, :, :, :, D:VB], 1.0)
            done = 2
            for i, (kind, w, bias, dst, n, k) in enumerate(loads):
                dve.wait_ge(w_loaded[i % 2], load_count[i])
                src = stage[i % 2][:, 0:n]
                if kind in ("full", "fc2"):
                    if kind == "full":
                        hi, lo = dst[:, k, :], dst[:, 2 + k, :]
                    else:
                        hi, lo = (dst[:, i_, k:k + 3, :].rearrange("p f c -> p (f c)") for i_ in range(2))
                    nc.vector.tensor_copy(hi, src).then_inc(w_hi, 1)
                    done += 1
                    dve.wait_ge(w_hi, done)
                    nc.vector.tensor_tensor(lo, src, hi.bitcast(F32), ALU.subtract).then_inc(w_split, 1)
                else:
                    to, m = (dst[0:KRB, 4, :], minus_lo[0:KRB, 0:1]) if kind == "rem" else (dst[:, :], minus_lo[0:2, 1:2])
                    src = src[0:to.shape[0]]
                    nc.vector.tensor_copy(to, src).then_inc(w_hi, 1)
                    done += 1
                    dve.wait_ge(w_hi, done)
                    nc.vector.scalar_tensor_tensor(to, to.bitcast(F32), m, src, ALU.mult, ALU.add).then_inc(w_split, 1)
            dve.wait_ge(w_split, len(loads))

            def normalise(src, stat, mv, var_eps, rs, dst, steps, rstd, b, ready):
                for t in range(NT):
                    ready(t)
                    last = nc.vector.bn_stats(stat[:, t, :], src[:, t, :])
                last.then_inc(steps, 1)
                dve.wait_ge(steps, b.times(4, 1))
                dve.sem_inc(passed, 1)
                for t in range(NT):
                    last = nc.vector.bn_aggr(mv[:, t, :], stat[:, t, :])
                last.then_inc(steps, 1)
                dve.wait_ge(steps, b.times(4, 2))
                nc.vector.tensor_scalar(var_eps[:, :], mv[:, :, 1], EPS, None, ALU.add).then_inc(steps, 1)
                dve.wait_ge(rstd, b.times(1, 1))
                for t in range(NT):
                    nc.vector.tensor_scalar(dst[:, t, 0:C], src[:, t, :], mv[:, t, 0:1], rs[:, t:t + 1],
                                            ALU.subtract, ALU.mult)
                    last = nc.vector.tensor_scalar(dst[:, t, C:CX].rearrange("p (r c) -> p r c", r=2),
                                                   src[:, t, 2 * P:C].unsqueeze(1).broadcast_to([P, 2, REM]),
                                                   mv[:, t, 0:1], rs[:, t:t + 1], ALU.subtract, ALU.mult)
                last.then_inc(steps, 1)

            def ln1(b, _):
                normalise(xin[:, b.par], stat1, mv1, ve1, rs1, xn, ln1_dve, rstd1, b,
                          lambda t: dve.wait_ge(x_loaded[b.par], b.pairs(16, 16)) if t == 0 else None)

            def remainder(v, xr, hi, rem, b):
                nc.vector.tensor_copy(xr[0:KR, :], v[0:KR, 2, :]).then_inc(hi, 1)
                dve.wait_ge(hi, b.times(2, 2))
                low = xr[2 * REM:KR, :]
                nc.vector.tensor_tensor(low, v[2 * REM:KR, 2, :], low.bitcast(F32), ALU.subtract).then_inc(rem, 1)

            def xt(b, n):
                dve.wait_ge(qkv_drained, b.times(QKV_USES, n + 1))
                if n == 0:
                    nc.vector.tensor_copy(xh1[:, :, :], v1[:, 0:2, :]).then_inc(x1_hi, 1)
                else:
                    remainder(v1, xr1, x1_hi, x1_rem, b)

            def qkv(b, n):
                t, w = divmod(n, 3)
                if w == 2:
                    return
                dve.wait_ge(qk_hi, b.times(2 * NT, 2 * t + w + 1))
                tile = (qs, ks)[w][:, b.par, t]
                hi, lo = (tile[:, :, 0:D], tile[:, :, 2 * D:KS]) if w == 0 else (tile[:, :, D:2 * D], tile[:, :, 0:D])
                nc.vector.tensor_tensor(lo, qkv_bank[:, 0:C].rearrange("p (h d) -> p h d", h=H), hi.bitcast(F32),
                                        ALU.subtract).then_inc(qkv_drained, 1)

            def s(b, j):
                for i in range(2):
                    dve.wait_ge(s_full[i], b.times(PAIRS, j + 1))
                    nc.vector.tensor_reduce(qs[:, b.par, :, 2 * j + i, KS:KSM],
                                            score_bank[i][:, :].rearrange("p (t l) -> p t l", t=NT),
                                            AX.X, ALU.max).then_inc(s_max[i], 1)

            def t2(b, j):
                dve.wait_ge(turn_full, b.times(TURN_USES, turn_use("t2", j) + 1))
                nc.vector.tensor_copy(q2[:, j % 2, :], turn_bank[:, 0:L]).then_inc(turn_drained, 1)

            def on(b, q):
                dve.wait_ge(turn_full, b.times(TURN_USES, turn_use("on", q) + 1))
                o = turn_bank[:, 0:NT * P].rearrange("p (t c v) -> p t c v", t=NT, c=4)
                nc.vector.reciprocal(rc[:, :, :, :], o[:, :, :, D:D + 1]).then_inc(recip, 1)
                dve.wait_ge(recip, b.times(QUADS, q + 1))
                to = onat[:, :, 4 * D * q:4 * D * (q + 1)].rearrange("p t (c d) -> p t c d", c=4)
                nc.vector.tensor_tensor(to, o[:, :, :, 0:D], rc[:, :, :, :].broadcast_to([P, NT, 4, D]), ALU.mult
                                        ).then_inc(turn_drained, 1)
                if q == QUADS - 1:
                    dve.wait_ge(turn_drained, b.times(TURN_USES, TURN_USES))
                    for t in range(NT):
                        last = nc.vector.tensor_copy(onat[:, t, C:CX].rearrange("p (r c) -> p r c", r=2),
                                                     onat[:, t, 2 * P:C].unsqueeze(1).broadcast_to([P, 2, REM]))
                    last.then_inc(o_ready, 1)

            def ot(b, n):
                dve.wait_ge(o_hi, b.times(2, n + 1))
                if n == 0:
                    nc.vector.tensor_tensor(xl3[:, :, :].rearrange("p c l -> p (c l)"), mlp_bank[:, :],
                                            xh3[:, :, :].rearrange("p c l -> p (c l)").bitcast(F32), ALU.subtract
                                            ).then_inc(mlp_drained, 1)
                else:
                    low = xr3[2 * REM:KR, :]
                    nc.vector.tensor_tensor(low, mlp_bank[2 * REM:KR, 0:L], low.bitcast(F32), ALU.subtract
                                            ).then_inc(mlp_drained, 1)

            def gated(b, t, use, which):
                wait(dve, summed, b.times(4, 2 * which + t - 1))
                dve.wait_ge(mlp_full, b.times(MLP_USES, use + t + 1))
                nc.vector.tensor_tensor(tmp[:, t, :], mlp_bank[:, 0:C], gate[:, b.par, which, :], ALU.mult
                                        ).then_inc(mlp_drained, 1)

            def proj(b, t):
                dve.wait_ge(gate_loaded[b.par], b.pairs(16, 16))
                gated(b, t, USE_PROJ, 0)

            def ln2(b, _):
                normalise(x1, stat2, mv2, ve2, rs2, xn2, ln2_dve, rstd2, b,
                          lambda t: dve.wait_ge(summed, b.times(4, 1 + t)))

            def lt(b, n):
                dve.wait_ge(mlp_drained, b.times(MLP_USES, USE_LT + n + 1))
                if n == 0:
                    nc.vector.tensor_copy(xh3[:, :, :], v3[:, 0:2, :]).then_inc(x3_hi, 1)
                else:
                    remainder(v3, xr3, x3_hi, x3_rem, b)

            def fc1(b, n):
                dve.wait_ge(mlp_drained, b.times(MLP_USES, USE_FC1 + n + 1))
                cols = slice(2 * L * n, min(2 * L * (n + 1), NF * L))
                nc.vector.tensor_copy(gh[:, cols], g[:, cols]).then_inc(g_hi, 1)

            def fc2(b, t):
                gated(b, t, USE_FC2, 1)

            run(dve, {"ln1": ln1, "xt": xt, "qkv": qkv, "s": s, "t2": t2, "on": on, "ot": ot, "proj": proj,
                      "ln2": ln2, "lt": lt, "fc1": fc1, "fc2": fc2})

        @block.gpsimd
        def _(pool):
            nc.gpsimd.memset(ident[:, :], 0.0).then_inc(iota_step, 1)
            pool.wait_ge(iota_step, 1)
            nc.gpsimd.affine_select(out=ident[:, :], in_=ident[:, :], compare_op=ALU.not_equal, fill=1.0, base=0,
                                    pattern=[[-1, P]], channel_multiplier=1).then_inc(iota_step, 1)
            nc.gpsimd.memset(qs[:, :, :, :, KS:HB].bitcast(F32), 0.0).then_inc(consts, 1)
            pool.wait_ge(mod_ready, 2)
            pool.wait_ge(w_split, len(loads))

            def ln1(b, _):
                wait(pool, qkv_drained, b.times(QKV_USES, 2 - QKV_USES))
                nc.gpsimd.tensor_copy(mod1[:, :], column(0, b)).then_inc(mod1_set, 1)
                pool.wait_ge(ln1_dve, b.times(4, 3))
                nc.gpsimd.tensor_tensor(rs1[:, :], ve1[:, :], mhalf[:, :], ALU.pow).then_inc(rstd1, 1)

            def ln2(b, _):
                wait(pool, mlp_drained, b.times(MLP_USES, USE_LT + 2 - MLP_USES))
                nc.gpsimd.tensor_copy(mod2[:, :], column(6, b)).then_inc(mod2_set, 1)
                pool.wait_ge(ln2_dve, b.times(4, 3))
                nc.gpsimd.tensor_tensor(rs2[:, :], ve2[:, :], mhalf[:, :], ALU.pow).then_inc(rstd2, 1)

            def column(v0, b):
                k = b.k if isinstance(b.half, int) else b.number()
                return mod[:, v0:v0 + 6, k:k + 1] if isinstance(k, int) else mod[:, v0:v0 + 6, bass.ds(k, 1)]

            def xt(b, n):
                if n == 0:
                    pool.wait_ge(x1_hi, b.times(2, 1))
                    nc.gpsimd.tensor_tensor(xl1[:, :, :], v1[:, 0:2, :], xh1[:, :, :].bitcast(F32), ALU.subtract
                                            ).then_inc(x1_lo, 1)

            def lt(b, n):
                if n == 0:
                    pool.wait_ge(x3_hi, b.times(2, 1))
                    nc.gpsimd.tensor_tensor(xl3[:, :, :], v3[:, 0:2, :], xh3[:, :, :].bitcast(F32), ALU.subtract
                                            ).then_inc(x3_lo, 1)

            def proj(b, t):
                pool.wait_ge(res_loaded, b.times(16, 16))
                wait(pool, stored, b.times(16, 0))
                pool.wait_ge(mlp_drained, b.times(MLP_USES, USE_PROJ + t + 1))
                nc.gpsimd.tensor_tensor(x1[:, t, :], tmp[:, t, :], xres[:, t, :], ALU.add).then_inc(summed, 1)

            def fc1(b, n):
                pool.wait_ge(g_hi, b.times(FU, n + 1))
                cols = slice(2 * L * n, min(2 * L * (n + 1), NF * L))
                nc.gpsimd.tensor_tensor(gl[:, cols], g[:, cols], gh[:, cols].bitcast(F32), ALU.subtract
                                        ).then_inc(g_lo, 1)

            def fc2(b, t):
                pool.wait_ge(mlp_drained, b.times(MLP_USES, USE_FC2 + t + 1))
                nc.gpsimd.tensor_tensor(x1[:, t, :], tmp[:, t, :], x1[:, t, :], ALU.add).then_inc(summed, 1)

            run(pool, {"ln1": ln1, "ln2": ln2, "xt": xt, "lt": lt, "proj": proj, "fc1": fc1, "fc2": fc2})


NAMES = ["x", "cond_1152", "L0_cond_W_qkv", "L0_cond_b_qkv", "L0_cond_W_proj", "L0_cond_b_proj", "L0_cond_W_fc1",
         "L0_cond_b_fc1", "L0_cond_W_fc2", "L0_cond_b_fc2", "L0_cond_W_ada", "L0_cond_b_ada"]


def kernel(**inputs):
    import numpy as np
    from concourse import bacc
    from concourse.bass_utils import run_bass_kernel_spmd

    nc = bacc.Bacc("TRN2", target_bir_lowering=False, num_devices=1)
    arrays, args = {}, []
    for name in NAMES:
        a = np.ascontiguousarray(inputs[name])
        arrays[f"in_{name}"] = a
        args.append(nc.dram_tensor(f"in_{name}", a.shape, mybir.dt.from_np(a.dtype), kind="ExternalInput").ap())
    args.append(nc.dram_tensor("out_0", (B, L, C), F32, kind="ExternalOutput").ap())
    args.append(nc.dram_tensor("gates", (B, 2, C), F32, kind="Internal").ap())
    dit_block(nc, *args)
    r = run_bass_kernel_spmd(nc, [arrays], core_ids=[0])
    return r.results[0]["out_0"]
```

```python
from contextlib import ExitStack

import concourse.bass as bass
from concourse import mybir
from concourse.alu_op_type import AluOpType as ALU

F32 = mybir.dt.float32
F32R = mybir.dt.float32r
ACT = mybir.ActivationFunctionType
AX = mybir.AxisListType

B, L, C = 32, 256, 288
H = 16
D = C // H
FF = 4 * C
EPS = 1e-6
P = 128
NT = L // P
REM = C - 2 * P
KR = 3 * REM
CX = C + 2 * REM
KRB = KR + 2
PAIRS = H // 2
QUADS = H // 4
HB = 64
KS = 3 * D
KSM = KS + 1
VB = 32
NF = FF // P
FU = (NF + 1) // 2
NV = 4
SCALE = float(D) ** -0.5

QKV_USES = 2 + 3 * NT
FU_ALT = FU // 2
MLP_USES = 2 + NT + 2 + (FU - FU_ALT) + NT
TURN_USES = 2 * QUADS
USE_PROJ, USE_LT, USE_FC1, USE_FC2 = 2, 2 + NT, 4 + NT, MLP_USES - NT

SCHEDULE = [
    ("t2", -1, 7),
    ("s", 0, 0), ("t1", 0, 1), ("xt", 1, 0), ("st", -1, 7), ("fc2", -2, 0), ("t2", 0, 0),
    ("s", 0, 1), ("pv", -1, 3), ("st", 0, 0), ("t1", 0, 2), ("on", -1, 3), ("xt", 1, 1), ("fc2", -2, 1),
    ("t2", 0, 1),
    ("s", 0, 2), ("t1", 0, 3), ("ot", -1, 0), ("qkv", 1, 0), ("st", 0, 1),
    ("s", 0, 3), ("t1", 0, 4), ("ot", -1, 1), ("t2", 0, 2), ("pv", 0, 0), ("st", 0, 2), ("on", 0, 0),
    ("proj", -1, 0), ("qkv", 1, 1), ("t2", 0, 3), ("proj", -1, 1),
    ("s", 0, 4), ("t1", 0, 5), ("st", 0, 3), ("ln2_stats", -1, 0), ("qkv", 1, 2), ("t2", 0, 4), ("pv", 0, 1),
    ("t1", 0, 6), ("st", 0, 4), ("ln2_apply", -1, 0),
    ("s", 0, 5), ("on", 0, 1), ("lt", -1, 0), ("qkv", 1, 3), ("t2", 0, 5), ("lt", -1, 1),
    ("s", 0, 6), ("t1", 0, 7), ("st", 0, 5), ("fc1", -1, 0), ("t2", 0, 6), ("fc1", -1, 1),
    ("s", 0, 7), ("ln1_stats", 2, 0), ("fc1", -1, 2), ("fc1", -1, 3), ("fc1", -1, 4), ("st", 0, 6), ("qkv", 1, 4),
    ("pv", 0, 2), ("t1", 1, 0), ("ln1_apply", 2, 0), ("on", 0, 2), ("qkv", 1, 5),
]

QKV_ORDER = [(0, 0), (0, 1), (1, 0), (1, 1), (0, 2), (1, 2)]
QK_USES = 2 + 4


class Batch:

    def __init__(self, half, k):
        self.half, self.k = half, k
        self.par = k % 2

    def times(self, n, plus):
        return self.half * (2 * n) + (self.k * n + plus)

    def pairs(self, n, plus):
        return self.half * n + (self.k // 2 * n + plus)

    def looped(self):
        return not isinstance(self.half, int)

    def number(self):
        return self.half * 2 + self.k


def wait(eng, sem, value):
    if not (isinstance(value, int) and value <= 0):
        eng.wait_ge(sem, value)


def run(eng, steps):
    def iteration(half, k, only=True):
        for name, off, n in SCHEDULE:
            if only and not 0 <= 2 * half + k + off < B:
                continue
            if name in steps:
                steps[name](Batch(half, k + off), n)

    for k in (-2, -1, 0, 1):
        iteration(0, k)
    with eng.Fori(1, B // 2 - 1) as half:
        for k in (0, 1):
            iteration(half, k, only=False)
    for k in range(B - 2, B + 2):
        iteration(0, k)


def dit_block(nc, x, cond, w_qkv, b_qkv, w_proj, b_proj, w_fc1, b_fc1, w_fc2, b_fc2, w_ada, b_ada, out, gates_dram):
    with ExitStack() as ctx:
        def sb(name, shape, dt=F32):
            return ctx.enter_context(nc.sbuf_tensor(name, shape, dt))

        def sem(name):
            return ctx.enter_context(nc.semaphore(name))

        score_bank = [ctx.enter_context(nc.psum_tensor(f"score_bank{t}", [P, 512], F32)) for t in range(2)]
        st_bank = ctx.enter_context(nc.psum_tensor("st_bank", [P, 2, NT, L], F32))
        t2_ps = st_bank[:, 0, 0, :]
        t1_bank = ctx.enter_context(nc.psum_tensor("t1_bank", [P, 512], F32))
        turn_bank = ctx.enter_context(nc.psum_tensor("turn_bank", [P, 512], F32))
        qkv_bank = ctx.enter_context(nc.psum_tensor("qkv_bank", [P, 512], F32))
        mlp_bank = ctx.enter_context(nc.psum_tensor("mlp_bank", [P, 512], F32))

        wq = sb("wq", [P, 5, 3 * C], F32R)
        wp = sb("wp", [P, 5, C], F32R)
        w1 = sb("w1", [P, 5, FF], F32R)
        w2 = sb("w2", [P, 2, NF, C], F32R)
        b2 = sb("b2", [2, C], F32R)
        ones_r = sb("ones_r", [2, P], F32R)
        ident = sb("ident", [P, P])
        ident_r = sb("ident_r", [P, P], F32R)
        minus_lo = sb("minus_lo", [P, 2])
        mhalf = sb("mhalf", [P, NT])
        mod = sb("mod", [P, NV * 3, B])
        xin = sb("xin", [P, 2, NT, C])
        xn = sb("xn", [P, NT, CX])
        mod1 = sb("mod1", [P, 6])
        stat1 = sb("stat1", [P, NT, 6])
        mv1 = sb("mv1", [P, NT, 2])
        ve1 = sb("ve1", [P, NT])
        rs1 = sb("rs1", [P, NT])
        v1 = sb("v1", [P, 3, L])
        xh1 = sb("xh1", [P, 2, L], F32R)
        xl1 = sb("xl1", [P, 2, L], F32R)
        xr1 = sb("xr1", [P, L], F32R)
        qs = sb("qs", [P, 2, NT, H, HB], F32R)
        ks = sb("ks", [P, 2, NT, H, HB], F32R)
        ve = sb("ve", [P, 2, NT, H, VB])
        qk1 = sb("qk1", [P, 4, 2, L], F32R)
        q2 = sb("q2", [P, 2, L], F32R)
        e = sb("e", [P, 4, 2, NT, L])
        ots = sb("ots", [P, L])
        rc = sb("rc", [P, NT, 4, 1])
        onat = sb("onat", [P, NT, CX])
        gate = sb("gate", [P, 2, 2, C])
        xres = sb("xres", [P, NT, C])
        tmp = sb("tmp", [P, NT, C])
        x1 = sb("x1", [P, NT, C])
        xn2 = sb("xn2", [P, NT, CX])
        mod2 = sb("mod2", [P, 6])
        stat2 = sb("stat2", [P, NT, 6])
        mv2 = sb("mv2", [P, NT, 2])
        ve2 = sb("ve2", [P, NT])
        rs2 = sb("rs2", [P, NT])
        v3 = sb("v3", [P, 3, L])
        xh3 = sb("xh3", [P, 2, L], F32R)
        xl3 = sb("xl3", [P, 2, L], F32R)
        xr3 = sb("xr3", [P, L], F32R)
        g = sb("g", [P, NF * L])
        gh = sb("gh", [P, NF * L], F32R)
        gl = sb("gl", [P, NF * L], F32R)

        consts = sem("consts")
        iota_step = sem("iota_step")
        w_loaded = [sem(f"w_loaded{i}") for i in range(2)]
        w_hi = sem("w_hi")
        w_split = sem("w_split")
        c_loaded = sem("c_loaded")
        ada_loaded = sem("ada_loaded")
        ada_exp = sem("ada_exp")
        silu_step = sem("silu_step")
        ada_turned = sem("ada_turned")
        ada_sT = sem("ada_sT")
        ada_mm = sem("ada_mm")
        ada_row = sem("ada_row")
        ada_step = sem("ada_step")
        mod_turned = sem("mod_turned")
        gates_ready = sem("gates_ready")
        mod_ready = sem("mod_ready")
        gates_stored = sem("gates_stored")
        x_loaded = [sem(f"x_loaded{i}") for i in range(2)]
        ln1_dve = sem("ln1_dve")
        rstd1 = sem("rstd1")
        mod1_set = sem("mod1_set")
        qkv_full = sem("qkv_full")
        qkv_drained = sem("qkv_drained")
        alt_full = sem("alt_full")
        alt_drained = sem("alt_drained")
        x1_hi = sem("x1_hi")
        x1_lo = sem("x1_lo")
        x1_rem = sem("x1_rem")
        qk_hi = sem("qk_hi")
        t1_full = sem("t1_full")
        t1_drained = sem("t1_drained")
        s_full = [sem(f"s_full{i}") for i in range(2)]
        s_max = [sem(f"s_max{i}") for i in range(2)]
        t2_full = sem("t2_full")
        q2_ready = sem("q2_ready")
        turn_full = sem("turn_full")
        turn_drained = sem("turn_drained")
        st_full = sem("st_full")
        e_ready = sem("e_ready")
        recip = sem("recip")
        gate_loaded = [sem(f"gate_loaded{i}") for i in range(2)]
        res_loaded = sem("res_loaded")
        mlp_full = sem("mlp_full")
        mlp_drained = sem("mlp_drained")
        o_ready = sem("o_ready")
        o_hi = sem("o_hi")
        summed = sem("summed")
        ln2_dve = sem("ln2_dve")
        rstd2 = sem("rstd2")
        mod2_set = sem("mod2_set")
        x3_hi = sem("x3_hi")
        x3_lo = sem("x3_lo")
        x3_rem = sem("x3_rem")
        g_hi = sem("g_hi")
        g_lo = sem("g_lo")
        stored = sem("stored")
        passed = sem("passed")

        stage = [g[:, 0:FF], g[:, FF:2 * FF]]
        loads = []
        for w, bias, dst, n in ((w_qkv, b_qkv, wq, 3 * C), (w_proj, b_proj, wp, C), (w_fc1, b_fc1, w1, FF)):
            loads += [("full", w, bias, dst, n, 0), ("full", w, bias, dst, n, 1), ("rem", w, bias, dst, n, 0)]
        loads += [("fc2", w_fc2, None, w2, 3 * C, f) for f in range(0, NF, 3)]
        loads.append(("b2", b_fc2, None, b2, C, 0))
        staged, load_count = [0, 0], []
        for i, load in enumerate(loads):
            staged[i % 2] += 16 * {"full": 1, "rem": 5, "fc2": 1, "b2": 2}[load[0]]
            load_count.append(staged[i % 2])

        K_ROWS = [(0, P), (P, P), (2 * P, REM)]
        e_flat = e[:, :, :, :, :].rearrange("p a b c d -> p (a b c d)")
        w_ada_sb = [e_flat[:, 0:6 * C], e_flat[:, 6 * C:12 * C],
                    ve[:, :, :, :, :].rearrange("p a b c d -> p (a b c d)")[0:REM, 0:6 * C]]
        c_in, c_exp = x1[0:B, 0, :], x1[0:B, 1, :]
        c_sig, c_silu = tmp[0:B, 0, :], tmp[0:B, 1, :]
        sT = onat[:, 0, 0:3 * B].rearrange("p (k b) -> p k b", k=3)
        MOD_OF = [0, 1, 3, 4]
        GATE_OF = [2, 5]
        ada_bank = [score_bank[0][:, :], score_bank[1][:, :], qkv_bank[:, :],
                    st_bank[:, 0, :, :].rearrange("p u l -> p (u l)"), st_bank[:, 1, :, :].rearrange("p u l -> p (u l)"),
                    mlp_bank[:, :]]
        mod_row = {0: xn[0:B, 0, :], 1: xn[0:B, 1, :], 3: xn2[0:B, 0, :], 4: xn2[0:B, 1, :]}
        gate_val = gate[0:B, 1, :, :]
        v1_row, v3_row = (v[0:B, :, :].rearrange("b c l -> b (c l)")[:, 0:2 * C] for v in (v1, v3))
        bias_row = {0: v1_row[:, 0:C], 1: v1_row[:, C:2 * C], 3: v3_row[:, 0:C], 4: v3_row[:, C:2 * C],
                    2: xres[0:B, 0, :], 5: xres[0:B, 1, :]}
        MOD_PS = turn_bank[:, 0:NV * 3 * B].rearrange("p (v b) -> p v b", b=B)
        N_ADA = 3 + 4

        def tiles_split_with(b, j):
            i = 3 + PAIRS * b.k + j
            return i if not b.looped() and i < len(loads) else None

        def products(xh, xl, xr, w):
            return [(xh[:, 0, :], w[:, 0, :]), (xh[:, 1, :], w[:, 1, :]), (xh[:, 0, :], w[:, 2, :]),
                    (xh[:, 1, :], w[:, 3, :]), (xl[:, 0, :], w[:, 0, :]), (xl[:, 1, :], w[:, 1, :]),
                    (xr[0:KRB, :], w[0:KRB, 4, :])]

        def fc1_use(b, n, plus=0):
            if n % 2:
                return qkv_bank, alt_full, alt_drained, b.times(FU_ALT, n // 2 + plus)
            return mlp_bank, mlp_full, mlp_drained, b.times(MLP_USES, USE_FC1 + n // 2 + plus)

        block = ctx.enter_context(nc.Block())

        @block.sync
        def _(sp):
            sp.dma_start(c_in, cond).then_inc(c_loaded, 16)
            for k, (r0, nr) in enumerate(K_ROWS):
                sp.dma_start(w_ada_sb[k], w_ada[r0:r0 + nr, :]).then_inc(ada_loaded, 16)
            for to, c0, n in ((v1_row, 0, 2 * C), (v3_row, 3 * C, 2 * C), (bias_row[2], 2 * C, C), (bias_row[5], 5 * C, C)):
                sp.dma_start(to, b_ada[c0:c0 + n].rearrange("(a c) -> a c", a=1).broadcast_to([B, n])
                             ).then_inc(ada_loaded, 16)

            def load_weights(i):
                kind, w, bias, dst, n, k = loads[i]
                if i >= 2:
                    sp.wait_ge(w_split, i - 1)
                s, to = w_loaded[i % 2], stage[i % 2]
                if kind == "full":
                    sp.dma_start(to[:, 0:n], w[k * P:(k + 1) * P, :]).then_inc(s, 16)
                elif kind == "rem":
                    for r in range(3):
                        sp.dma_start(to[REM * r:REM * (r + 1), 0:n], w[2 * P:C, :]).then_inc(s, 16)
                    for r in range(2):
                        sp.dma_start(to[KR + r:KR + r + 1, 0:n], bias.rearrange("(a n) -> a n", a=1)).then_inc(s, 16)
                elif kind == "fc2":
                    sp.dma_start(to[:, 0:n].rearrange("p (f c) -> p f c", f=3),
                                 w[k * P:(k + 3) * P, :].rearrange("(f p) c -> p f c", p=P)).then_inc(s, 16)
                else:
                    for r in range(2):
                        sp.dma_start(to[r:r + 1, 0:n], w.rearrange("(a n) -> a n", a=1)).then_inc(s, 16)

            for i in range(3):
                load_weights(i)

            def row(ap, b):
                return ap[b.k] if isinstance(b.half, int) and b.half == 0 else ap[b.number()]

            def load_x(b, _):
                wait(sp, ln1_dve, b.times(4, -4))
                sp.dma_start(xin[:, b.par], row(x, b).rearrange("(p t) c -> p t c", t=NT)
                             ).then_inc(x_loaded[b.par], 16)

            def load_residual(b, n):
                if n:
                    return
                if not b.looped() and b.k == 0:
                    sp.wait_ge(gates_ready, 2)
                    sp.dma_start(gates_dram, gate_val).then_inc(gates_stored, 16)
                    sp.wait_ge(gates_stored, 16)
                wait(sp, summed, b.times(4, -2))
                sp.dma_start(xres[:, :, :], row(x, b).rearrange("(p t) c -> p t c", t=NT)
                             ).then_inc(res_loaded, 16)
                sp.dma_start(gate[:, b.par], row(gates_dram, b).unsqueeze(0).broadcast_to([P, 2, C])
                             ).then_inc(gate_loaded[b.par], 16)

            def store(b, n):
                if n == NT - 1:
                    sp.wait_ge(summed, b.times(4, 4))
                    sp.dma_start(row(out, b).rearrange("(p t) c -> p t c", t=NT), x1[:, :, :]).then_inc(stored, 16)

            def more_weights(b, j):
                i = tiles_split_with(b, j)
                if i is not None:
                    load_weights(i)

            run(sp, {"ln1_stats": load_x, "ot": load_residual, "fc2": store, "s": more_weights})
            sp.wait_ge(stored, 16 * B)

        @block.tensor
        def _(pe):
            pe.wait_ge(iota_step, 2)
            pe.wait_ge(silu_step, 3)
            for k, (r0, nr) in enumerate(K_ROWS):
                last = nc.tensor.transpose(t1_bank[0:nr, k * B:(k + 1) * B], c_silu[:, r0:r0 + nr], ident[0:B, 0:B])
            last.then_inc(ada_turned, 1)
            pe.wait_ge(ada_sT, 1)
            pe.wait_ge(ada_loaded, 16 * N_ADA)
            for v in range(6):
                for k, (_r, nr) in enumerate(K_ROWS):
                    last = nc.tensor.matmul(ada_bank[v][0:B, 0:C], sT[0:nr, k, :], w_ada_sb[k][:, v * C:(v + 1) * C],
                                            start=(k == 0), stop=(k == 2))
                last.then_inc(ada_mm, 1)
            pe.wait_ge(ada_step, 2)
            for i, v in enumerate(MOD_OF):
                for tile, width in enumerate((P, P, KR)):
                    last = nc.tensor.transpose(MOD_PS[0:width, 3 * i + tile, :], mod_row[v][:, tile * P:tile * P + width],
                                               ident[0:B, 0:B])
            last.then_inc(mod_turned, 1)
            pe.wait_ge(gates_ready, 2)
            pe.wait_ge(mod_ready, 1)
            pe.wait_ge(consts, 2)
            pe.wait_ge(w_split, 3)

            def need_weights(b, n):
                if not b.looped() and b.k == 0:
                    pe.wait_ge(w_split, n)

            def turn_x(bank, xn_, n):
                for t in range(NT):
                    if n == 0:
                        for c in range(2):
                            last = nc.tensor.transpose(bank[:, c * L + t * P:c * L + (t + 1) * P],
                                                       xn_[:, t, c * P:(c + 1) * P], ident[:, :])
                    else:
                        last = nc.tensor.transpose(bank[0:KR, t * P:(t + 1) * P], xn_[:, t, 2 * P:CX],
                                                   ident[:, :])
                return last

            def xt(b, n):
                pe.wait_ge(ln1_dve, b.times(4, 4))
                wait(pe, qkv_drained, b.times(QKV_USES, n))
                turn_x(qkv_bank, xn, n).then_inc(qkv_full, 1)

            def qkv(b, n):
                t, w = QKV_ORDER[n]
                pe.wait_ge(x1_lo, b.times(1, 1))
                pe.wait_ge(x1_rem, b.times(1, 1))
                pe.wait_ge(qkv_drained, b.times(QKV_USES, 2 + n))
                if w == 2:
                    wait(pe, alt_drained, b.times(FU_ALT, -FU_ALT))
                pr = products(xh1, xl1, xr1, wq)
                for i, (xa, wa) in enumerate(pr):
                    last = nc.tensor.matmul(qkv_bank[:, 0:C], xa[:, t * P:(t + 1) * P], wa[:, w * C:(w + 1) * C],
                                            start=(i == 0), stop=(i == len(pr) - 1))
                last.then_inc(qkv_full, 1)

            def t1(b, j):
                if j == 0:
                    pe.wait_ge(qkv_drained, b.times(QKV_USES, QK_USES))
                wait(pe, t1_drained, b.times(PAIRS, j))
                for i, src in enumerate((qs, ks)):
                    for t in range(NT):
                        last = nc.tensor.transpose(t1_bank[:, i * L + t * P:i * L + (t + 1) * P].bitcast(F32R),
                                                   src[:, b.par, t, 2 * j:2 * j + 2, :], ident_r[:, :])
                last.then_inc(t1_full, 1)

            def s(b, j):
                pe.wait_ge(t1_drained, b.times(PAIRS, j + 1))
                for i in range(2):
                    wait(pe, s_max[i], b.times(PAIRS, j))
                    rows = slice(HB * i, HB * i + KS)
                    for t in range(NT):
                        last = nc.tensor.matmul(score_bank[i][:, t * L:(t + 1) * L],
                                                qk1[rows, j % 4, 0, t * P:(t + 1) * P], qk1[rows, j % 4, 1, :],
                                                start=True, stop=True)
                    last.then_inc(s_full[i], 1)

            def t2(b, j):
                for i in range(2):
                    pe.wait_ge(s_max[i], b.times(PAIRS, j + 1))
                wait(pe, e_ready, b.times(PAIRS, j))
                for t in range(NT):
                    last = nc.tensor.transpose(t2_ps[:, t * P:(t + 1) * P].bitcast(F32R),
                                               qs[:, b.par, t, 2 * j:2 * j + 2, :], ident_r[:, :])
                last.then_inc(t2_full, 1)

            def st(b, j):
                pe.wait_ge(q2_ready, b.times(PAIRS, j + 1))
                for i in range(2):
                    rows = slice(HB * i, HB * i + KSM)
                    for u in range(NT):
                        last = nc.tensor.matmul(st_bank[:, i, u, :], qk1[rows, j % 4, 1, u * P:(u + 1) * P],
                                                q2[rows, j % 2, :], start=True, stop=True)
                last.then_inc(st_full, 1)

            def pv(b, q):
                pe.wait_ge(e_ready, b.times(PAIRS, 2 * q + 2))
                if q == 0:
                    pe.wait_ge(qkv_drained, b.times(QKV_USES, QKV_USES))
                wait(pe, turn_drained, b.times(TURN_USES, 2 * q))
                for u in range(NT):
                    for c in range(4):
                        last = nc.tensor.matmul(turn_bank[VB * c:VB * (c + 1), 0:L], ve[:, b.par, u, 4 * q + c, :],
                                                e[:, 2 * (q % 2) + c // 2, c % 2, u, :],
                                                start=(u == 0), stop=(u == NT - 1))
                last.then_inc(turn_full, 1)

            def on(b, q):
                pe.wait_ge(turn_drained, b.times(TURN_USES, 2 * q + 1))
                for t in range(NT):
                    last = nc.tensor.transpose(turn_bank[:, t * P:(t + 1) * P], ots[:, t * P:(t + 1) * P], ident[:, :])
                last.then_inc(turn_full, 1)

            def ot(b, n):
                pe.wait_ge(o_ready, b.times(1, 1))
                wait(pe, mlp_drained, b.times(MLP_USES, n))
                turn_x(mlp_bank, onat, n).then_inc(mlp_full, 1)

            def proj(b, t):
                need_weights(b, 6)
                pe.wait_ge(mlp_drained, b.times(MLP_USES, USE_PROJ + t))
                pr = products(xh3, xl3, xr3, wp)
                for i, (xa, wa) in enumerate(pr):
                    last = nc.tensor.matmul(mlp_bank[:, 0:C], xa[:, t * P:(t + 1) * P], wa,
                                            start=(i == 0), stop=(i == len(pr) - 1))
                last.then_inc(mlp_full, 1)

            def lt(b, n):
                pe.wait_ge(ln2_dve, b.times(4, 4))
                pe.wait_ge(mlp_drained, b.times(MLP_USES, USE_LT + n))
                turn_x(mlp_bank, xn2, n).then_inc(mlp_full, 1)

            def fc1(b, n):
                pe.wait_ge(x3_lo, b.times(1, 1))
                pe.wait_ge(x3_rem, b.times(1, 1))
                need_weights(b, 9)
                bank, full, drained, use = fc1_use(b, n)
                wait(pe, drained, use)
                if n % 2:
                    qk_done = b.times(QKV_USES, 2 * QKV_USES + QK_USES)
                    pe.wait_ge(qkv_drained, qk_done if b.looped() else min(qk_done, B * QKV_USES))
                for f in range(2 * n, min(2 * n + 2, NF)):
                    pr = products(xh3, xl3, xr3, w1)
                    for i, (xa, wa) in enumerate(pr):
                        last = nc.tensor.matmul(bank[:, (f % 2) * L:(f % 2 + 1) * L], wa[:, f * P:(f + 1) * P], xa,
                                                start=(i == 0), stop=(i == len(pr) - 1))
                last.then_inc(full, 1)

            def fc2(b, t):
                need_weights(b, len(loads))
                pe.wait_ge(g_lo, b.times(FU, FU))
                pe.wait_ge(mlp_drained, b.times(MLP_USES, USE_FC2 + t))
                nc.tensor.matmul(mlp_bank[:, 0:C], ones_r[:, :], b2[:, :], start=True, stop=False)
                for f in range(NF):
                    cols = slice(f * L + t * P, f * L + (t + 1) * P)
                    nc.tensor.matmul(mlp_bank[:, 0:C], gh[:, cols], w2[:, 0, f, :], start=False, stop=False)
                    nc.tensor.matmul(mlp_bank[:, 0:C], gh[:, cols], w2[:, 1, f, :], start=False, stop=False)
                    last = nc.tensor.matmul(mlp_bank[:, 0:C], gl[:, cols], w2[:, 0, f, :], start=False,
                                            stop=(f == NF - 1))
                last.then_inc(mlp_full, 1)

            run(pe, {"xt": xt, "qkv": qkv, "t1": t1, "s": s, "t2": t2, "st": st, "pv": pv, "on": on, "ot": ot,
                     "proj": proj, "lt": lt, "fc1": fc1, "fc2": fc2})

        @block.scalar
        def _(act):
            act.wait_ge(c_loaded, 16)
            nc.scalar.activation(c_exp, c_in, ACT.Exp, scale=-1.0).then_inc(ada_exp, 1)
            act.wait_ge(mod_ready, 1)

            def xt(b, n):
                pe_use = b.times(QKV_USES, n + 1)
                act.wait_ge(mod1_set, b.times(1, 1))
                if n == 0:
                    wait(act, x1_lo, b.times(1, 0))
                    wait(act, x1_rem, b.times(1, 0))
                act.wait_ge(qkv_full, pe_use)
                for c in (0, 1) if n == 0 else (2,):
                    rows = P if c < 2 else KR
                    last = nc.scalar.activation(v1[0:rows, c, :], qkv_bank[0:rows, (c % 2) * L:(c % 2 + 1) * L],
                                                ACT.Identity, bias=mod1[0:rows, c:c + 1], scale=mod1[0:rows, 3 + c:4 + c])
                last.then_inc(qkv_drained, 1)

            def qkv(b, n):
                t, w = QKV_ORDER[n]
                act.wait_ge(qkv_full, b.times(QKV_USES, 3 + n))
                src = qkv_bank[:, 0:C].rearrange("p (h d) -> p h d", h=H)
                if w == 2:
                    nc.scalar.copy(ve[:, b.par, t, :, 0:D], src).then_inc(qkv_drained, 1)
                else:
                    to = (qs[:, b.par, t, :, 0:2 * D], ks[:, b.par, t, :, D:KS])[w]
                    nc.scalar.copy(to.rearrange("p h (r d) -> p h r d", r=2),
                                   src.unsqueeze(2).broadcast_to([P, H, 2, D])).then_inc(qk_hi, 1)

            def t1(b, j):
                act.wait_ge(t1_full, b.times(PAIRS, j + 1))
                nc.scalar.copy(qk1[:, j % 4, :, :].rearrange("p i l -> p (i l)"), t1_bank[:, :]).then_inc(t1_drained, 1)

            def st(b, j):
                act.wait_ge(st_full, b.times(PAIRS, j + 1))
                nc.scalar.activation(e[:, j % 4, :, :, :].rearrange("p i u l -> p (i u l)"),
                                     st_bank[:, :, :, :].rearrange("p i u l -> p (i u l)"),
                                     ACT.Exp, scale=SCALE).then_inc(e_ready, 1)

            def pv(b, q):
                act.wait_ge(turn_full, b.times(TURN_USES, 2 * q + 1))
                nc.scalar.copy(ots[:, :], turn_bank[:, 0:L]).then_inc(turn_drained, 1)

            def ot(b, n):
                act.wait_ge(mlp_full, b.times(MLP_USES, n + 1))
                if n == 0:
                    nc.scalar.copy(xh3[:, :, :].rearrange("p c l -> p (c l)"), mlp_bank[:, :]).then_inc(o_hi, 1)
                else:
                    nc.scalar.copy(xr3[0:KR, :], mlp_bank[0:KR, 0:L]).then_inc(o_hi, 1)

            def lt(b, n):
                act.wait_ge(mod2_set, b.times(1, 1))
                if n == 0:
                    wait(act, x3_lo, b.times(1, 0))
                    wait(act, x3_rem, b.times(1, 0))
                act.wait_ge(mlp_full, b.times(MLP_USES, USE_LT + n + 1))
                for c in (0, 1) if n == 0 else (2,):
                    rows = P if c < 2 else KR
                    last = nc.scalar.activation(v3[0:rows, c, :], mlp_bank[0:rows, (c % 2) * L:(c % 2 + 1) * L],
                                                ACT.Identity, bias=mod2[0:rows, c:c + 1], scale=mod2[0:rows, 3 + c:4 + c])
                last.then_inc(mlp_drained, 1)

            def fc1(b, n):
                wait(act, g_lo, b.times(FU, n + 1 - FU))
                if not b.looped() and b.k == 0:
                    act.wait_ge(w_split, len(loads))
                bank, full, drained, count = fc1_use(b, n, 1)
                act.wait_ge(full, count)
                cols = min(2 * L, NF * L - 2 * L * n)
                nc.scalar.activation(g[:, 2 * L * n:2 * L * n + cols], bank[:, 0:cols], ACT.Gelu_apprx_tanh
                                     ).then_inc(drained, 1)

            run(act, {"xt": xt, "qkv": qkv, "t1": t1, "st": st, "pv": pv, "ot": ot, "lt": lt, "fc1": fc1})

        @block.vector
        def _(dve):
            nc.vector.memset(mod[:, :, :], 0.0)
            nc.vector.memset(minus_lo[:, :], 0.0).then_inc(w_hi, 1)
            dve.wait_ge(w_hi, 1)
            nc.vector.memset(minus_lo[REM:2 * REM, 0:1], -1.0)
            nc.vector.memset(minus_lo[KR:P, 0:1], -1.0)
            nc.vector.memset(minus_lo[0:REM, 1:2], -1.0).then_inc(w_hi, 1)
            dve.wait_ge(w_hi, 2)
            nc.vector.memset(minus_lo[KR:KR + 1, 0:1], 0.0)
            nc.vector.memset(minus_lo[0:1, 1:2], 0.0)
            nc.vector.memset(mhalf[:, :], -0.5)
            nc.vector.memset(ones_r[:, :].bitcast(F32), 1.0)
            nc.vector.memset(xr1[KR:KRB, :].bitcast(F32), 1.0)
            nc.vector.memset(xr3[KR:KRB, :].bitcast(F32), 1.0)
            dve.wait_ge(iota_step, 2)
            nc.vector.tensor_copy(ident_r[:, :], ident[:, :])
            dve.wait_ge(c_loaded, 16)
            dve.wait_ge(ada_exp, 1)
            nc.vector.tensor_scalar(c_exp, c_exp, 1.0, None, ALU.add).then_inc(silu_step, 1)
            dve.wait_ge(silu_step, 1)
            nc.vector.reciprocal(c_sig, c_exp).then_inc(silu_step, 1)
            dve.wait_ge(silu_step, 2)
            nc.vector.tensor_tensor(c_silu, c_in, c_sig, ALU.mult).then_inc(silu_step, 1)
            dve.wait_ge(ada_turned, 1)
            nc.vector.tensor_copy(sT[:, 0:2, :], t1_bank[:, 0:2 * B].rearrange("p (k b) -> p k b", k=2))
            nc.vector.tensor_copy(sT[0:REM, 2, :], t1_bank[0:REM, 2 * B:3 * B]).then_inc(ada_sT, 1)
            nc.vector.memset(ks[:, :, :, :, KSM:HB].bitcast(F32), 0.0)
            nc.vector.memset(ks[:, :, :, :, KS:KSM].bitcast(F32), -1.0).then_inc(consts, 1)
            dve.wait_ge(ada_loaded, 16 * N_ADA)
            for v in range(6):
                dve.wait_ge(ada_mm, v + 1)
                if v in GATE_OF:
                    nc.vector.tensor_tensor(gate_val[:, v // 3, :], ada_bank[v][0:B, 0:C], bias_row[v], ALU.add
                                            ).then_inc(gates_ready, 1)
                else:
                    nc.vector.scalar_tensor_tensor(mod_row[v][:, 0:C], ada_bank[v][0:B, 0:C], float(v % 3), bias_row[v],
                                                   ALU.add, ALU.add).then_inc(ada_row, 1)
            dve.wait_ge(ada_row, NV)
            for i, rows in enumerate((xn, xn2)):
                nc.vector.tensor_copy(rows[0:B, :, C:CX].rearrange("b v (r c) -> b v r c", r=2),
                                      rows[0:B, :, 2 * P:C].unsqueeze(2).broadcast_to([B, 2, 2, REM])).then_inc(ada_step, 1)
            nc.vector.memset(ve[:, :, :, :, D:VB], 1.0)
            dve.wait_ge(mod_turned, 1)
            mod4 = mod[:, :, :].rearrange("p (v c) b -> p v c b", c=3)
            ps4 = MOD_PS.rearrange("p (v c) b -> p v c b", c=3)
            nc.vector.tensor_copy(mod4[:, :, 0:2, :], ps4[:, :, 0:2, :])
            nc.vector.tensor_copy(mod4[0:KR, :, 2, :], ps4[0:KR, :, 2, :]).then_inc(mod_ready, 1)

            def split_weights(i):
                kind, w, bias, dst, n, k = loads[i]
                dve.wait_ge(w_loaded[i % 2], load_count[i])
                src = stage[i % 2][:, 0:n]
                if kind in ("full", "fc2"):
                    if kind == "full":
                        hi, lo = dst[:, k, :], dst[:, 2 + k, :]
                    else:
                        hi, lo = (dst[:, i_, k:k + 3, :].rearrange("p f c -> p (f c)") for i_ in range(2))
                    nc.vector.tensor_copy(hi, src).then_inc(w_hi, 1)
                    dve.wait_ge(w_hi, 3 + i)
                    nc.vector.tensor_tensor(lo, src, hi.bitcast(F32), ALU.subtract).then_inc(w_split, 1)
                else:
                    to, m = (dst[0:KRB, 4, :], minus_lo[0:KRB, 0:1]) if kind == "rem" else (dst[:, :], minus_lo[0:2, 1:2])
                    src = src[0:to.shape[0]]
                    nc.vector.tensor_copy(to, src).then_inc(w_hi, 1)
                    dve.wait_ge(w_hi, 3 + i)
                    nc.vector.scalar_tensor_tensor(to, to.bitcast(F32), m, src, ALU.mult, ALU.add).then_inc(w_split, 1)

            for i in range(3):
                split_weights(i)

            def statistics(src, stat, mv, var_eps, steps, b, ready):
                for t in range(NT):
                    ready(t)
                    last = nc.vector.bn_stats(stat[:, t, :], src[:, t, :])
                last.then_inc(steps, 1)
                dve.wait_ge(steps, b.times(4, 1))
                dve.sem_inc(passed, 1)
                for t in range(NT):
                    last = nc.vector.bn_aggr(mv[:, t, :], stat[:, t, :])
                last.then_inc(steps, 1)
                dve.wait_ge(steps, b.times(4, 2))
                nc.vector.tensor_scalar(var_eps[:, :], mv[:, :, 1], EPS, None, ALU.add).then_inc(steps, 1)

            def normalise(src, mv, rs, dst, steps, rstd, b):
                dve.wait_ge(rstd, b.times(1, 1))
                for t in range(NT):
                    nc.vector.tensor_scalar(dst[:, t, 0:C], src[:, t, :], mv[:, t, 0:1], rs[:, t:t + 1],
                                            ALU.subtract, ALU.mult)
                    last = nc.vector.tensor_scalar(dst[:, t, C:CX].rearrange("p (r c) -> p r c", r=2),
                                                   src[:, t, 2 * P:C].unsqueeze(1).broadcast_to([P, 2, REM]),
                                                   mv[:, t, 0:1], rs[:, t:t + 1], ALU.subtract, ALU.mult)
                last.then_inc(steps, 1)

            def ln1_stats(b, _):
                statistics(xin[:, b.par], stat1, mv1, ve1, ln1_dve, b,
                           lambda t: dve.wait_ge(x_loaded[b.par], b.pairs(16, 16)) if t == 0 else None)

            def ln1_apply(b, _):
                normalise(xin[:, b.par], mv1, rs1, xn, ln1_dve, rstd1, b)

            def remainder(v, xr, hi, rem, b):
                nc.vector.tensor_copy(xr[0:KR, :], v[0:KR, 2, :]).then_inc(hi, 1)
                dve.wait_ge(hi, b.times(2, 2))
                low = xr[2 * REM:KR, :]
                nc.vector.tensor_tensor(low, v[2 * REM:KR, 2, :], low.bitcast(F32), ALU.subtract).then_inc(rem, 1)

            def xt(b, n):
                dve.wait_ge(qkv_drained, b.times(QKV_USES, n + 1))
                if n == 0:
                    nc.vector.tensor_copy(xh1[:, :, :], v1[:, 0:2, :]).then_inc(x1_hi, 1)
                else:
                    remainder(v1, xr1, x1_hi, x1_rem, b)

            def qkv(b, n):
                t, w = QKV_ORDER[n]
                if w == 2:
                    return
                dve.wait_ge(qk_hi, b.times(2 * NT, 2 * t + w + 1))
                tile = (qs, ks)[w][:, b.par, t]
                hi, lo = (tile[:, :, 0:D], tile[:, :, 2 * D:KS]) if w == 0 else (tile[:, :, D:2 * D], tile[:, :, 0:D])
                nc.vector.tensor_tensor(lo, qkv_bank[:, 0:C].rearrange("p (h d) -> p h d", h=H), hi.bitcast(F32),
                                        ALU.subtract).then_inc(qkv_drained, 1)

            def s(b, j):
                for i in range(2):
                    dve.wait_ge(s_full[i], b.times(PAIRS, j + 1))
                    nc.vector.tensor_reduce(qs[:, b.par, :, 2 * j + i, KS:KSM],
                                            score_bank[i][:, :].rearrange("p (t l) -> p t l", t=NT),
                                            AX.X, ALU.max).then_inc(s_max[i], 1)
                i = tiles_split_with(b, j)
                if i is not None:
                    split_weights(i)

            def t2(b, j):
                dve.wait_ge(t2_full, b.times(PAIRS, j + 1))
                nc.vector.tensor_copy(q2[:, j % 2, :], t2_ps).then_inc(q2_ready, 1)

            def on(b, q):
                dve.wait_ge(turn_full, b.times(TURN_USES, 2 * q + 1 + 1))
                o = turn_bank[:, 0:NT * P].rearrange("p (t c v) -> p t c v", t=NT, c=4)
                nc.vector.reciprocal(rc[:, :, :, :], o[:, :, :, D:D + 1]).then_inc(recip, 1)
                dve.wait_ge(recip, b.times(QUADS, q + 1))
                to = onat[:, :, 4 * D * q:4 * D * (q + 1)].rearrange("p t (c d) -> p t c d", c=4)
                nc.vector.tensor_tensor(to, o[:, :, :, 0:D], rc[:, :, :, :].broadcast_to([P, NT, 4, D]), ALU.mult
                                        ).then_inc(turn_drained, 1)
                if q == QUADS - 1:
                    dve.wait_ge(turn_drained, b.times(TURN_USES, TURN_USES))
                    for t in range(NT):
                        last = nc.vector.tensor_copy(onat[:, t, C:CX].rearrange("p (r c) -> p r c", r=2),
                                                     onat[:, t, 2 * P:C].unsqueeze(1).broadcast_to([P, 2, REM]))
                    last.then_inc(o_ready, 1)

            def ot(b, n):
                dve.wait_ge(o_hi, b.times(2, n + 1))
                if n == 0:
                    nc.vector.tensor_tensor(xl3[:, :, :].rearrange("p c l -> p (c l)"), mlp_bank[:, :],
                                            xh3[:, :, :].rearrange("p c l -> p (c l)").bitcast(F32), ALU.subtract
                                            ).then_inc(mlp_drained, 1)
                else:
                    low = xr3[2 * REM:KR, :]
                    nc.vector.tensor_tensor(low, mlp_bank[2 * REM:KR, 0:L], low.bitcast(F32), ALU.subtract
                                            ).then_inc(mlp_drained, 1)

            def gated(b, t, use, which):
                wait(dve, summed, b.times(4, 2 * which + t - 1))
                dve.wait_ge(mlp_full, b.times(MLP_USES, use + t + 1))
                nc.vector.tensor_tensor(tmp[:, t, :], mlp_bank[:, 0:C], gate[:, b.par, which, :], ALU.mult
                                        ).then_inc(mlp_drained, 1)

            def proj(b, t):
                dve.wait_ge(gate_loaded[b.par], b.pairs(16, 16))
                gated(b, t, USE_PROJ, 0)

            def ln2_stats(b, _):
                statistics(x1, stat2, mv2, ve2, ln2_dve, b, lambda t: dve.wait_ge(summed, b.times(4, 1 + t)))

            def ln2_apply(b, _):
                normalise(x1, mv2, rs2, xn2, ln2_dve, rstd2, b)

            def lt(b, n):
                dve.wait_ge(mlp_drained, b.times(MLP_USES, USE_LT + n + 1))
                if n == 0:
                    nc.vector.tensor_copy(xh3[:, :, :], v3[:, 0:2, :]).then_inc(x3_hi, 1)
                else:
                    remainder(v3, xr3, x3_hi, x3_rem, b)

            def fc1(b, n):
                _bank, _full, drained, count = fc1_use(b, n, 1)
                dve.wait_ge(drained, count)
                cols = slice(2 * L * n, min(2 * L * (n + 1), NF * L))
                nc.vector.tensor_copy(gh[:, cols], g[:, cols]).then_inc(g_hi, 1)

            def fc2(b, t):
                gated(b, t, USE_FC2, 1)

            run(dve, {"ln1_stats": ln1_stats, "ln1_apply": ln1_apply, "xt": xt, "qkv": qkv, "s": s, "t2": t2, "on": on,
                      "ot": ot, "proj": proj, "ln2_stats": ln2_stats, "ln2_apply": ln2_apply, "lt": lt, "fc1": fc1,
                      "fc2": fc2})

        @block.gpsimd
        def _(pool):
            nc.gpsimd.memset(ident[:, :], 0.0).then_inc(iota_step, 1)
            pool.wait_ge(iota_step, 1)
            nc.gpsimd.affine_select(out=ident[:, :], in_=ident[:, :], compare_op=ALU.not_equal, fill=1.0, base=0,
                                    pattern=[[-1, P]], channel_multiplier=1).then_inc(iota_step, 1)
            nc.gpsimd.memset(qs[:, :, :, :, KS:HB].bitcast(F32), 0.0).then_inc(consts, 1)
            pool.wait_ge(mod_ready, 1)

            def ln1(b, _):
                wait(pool, qkv_drained, b.times(QKV_USES, 2 - QKV_USES))
                nc.gpsimd.tensor_copy(mod1[:, :], column(0, b)).then_inc(mod1_set, 1)
                pool.wait_ge(ln1_dve, b.times(4, 3))
                nc.gpsimd.tensor_tensor(rs1[:, :], ve1[:, :], mhalf[:, :], ALU.pow).then_inc(rstd1, 1)

            def ln2(b, _):
                wait(pool, mlp_drained, b.times(MLP_USES, USE_LT + 2 - MLP_USES))
                nc.gpsimd.tensor_copy(mod2[:, :], column(6, b)).then_inc(mod2_set, 1)
                pool.wait_ge(ln2_dve, b.times(4, 3))
                nc.gpsimd.tensor_tensor(rs2[:, :], ve2[:, :], mhalf[:, :], ALU.pow).then_inc(rstd2, 1)

            def column(v0, b):
                k = b.k if isinstance(b.half, int) else b.number()
                return mod[:, v0:v0 + 6, k:k + 1] if isinstance(k, int) else mod[:, v0:v0 + 6, bass.ds(k, 1)]

            def xt(b, n):
                if n == 0:
                    pool.wait_ge(x1_hi, b.times(2, 1))
                    nc.gpsimd.tensor_tensor(xl1[:, :, :], v1[:, 0:2, :], xh1[:, :, :].bitcast(F32), ALU.subtract
                                            ).then_inc(x1_lo, 1)

            def lt(b, n):
                if n == 0:
                    pool.wait_ge(x3_hi, b.times(2, 1))
                    nc.gpsimd.tensor_tensor(xl3[:, :, :], v3[:, 0:2, :], xh3[:, :, :].bitcast(F32), ALU.subtract
                                            ).then_inc(x3_lo, 1)

            def proj(b, t):
                pool.wait_ge(res_loaded, b.times(16, 16))
                wait(pool, stored, b.times(16, 0))
                pool.wait_ge(mlp_drained, b.times(MLP_USES, USE_PROJ + t + 1))
                nc.gpsimd.tensor_tensor(x1[:, t, :], tmp[:, t, :], xres[:, t, :], ALU.add).then_inc(summed, 1)

            def fc1(b, n):
                pool.wait_ge(g_hi, b.times(FU, n + 1))
                cols = slice(2 * L * n, min(2 * L * (n + 1), NF * L))
                nc.gpsimd.tensor_tensor(gl[:, cols], g[:, cols], gh[:, cols].bitcast(F32), ALU.subtract
                                        ).then_inc(g_lo, 1)

            def fc2(b, t):
                pool.wait_ge(mlp_drained, b.times(MLP_USES, USE_FC2 + t + 1))
                nc.gpsimd.tensor_tensor(x1[:, t, :], tmp[:, t, :], x1[:, t, :], ALU.add).then_inc(summed, 1)

            run(pool, {"ln1_stats": ln1, "ln2_stats": ln2, "xt": xt, "lt": lt, "proj": proj, "fc1": fc1, "fc2": fc2})


NAMES = ["x", "cond_1152", "L0_cond_W_qkv", "L0_cond_b_qkv", "L0_cond_W_proj", "L0_cond_b_proj", "L0_cond_W_fc1",
         "L0_cond_b_fc1", "L0_cond_W_fc2", "L0_cond_b_fc2", "L0_cond_W_ada", "L0_cond_b_ada"]


def kernel(**inputs):
    import numpy as np
    from concourse import bacc
    from concourse.bass_utils import run_bass_kernel_spmd

    nc = bacc.Bacc("TRN2", target_bir_lowering=False, num_devices=1)
    arrays, args = {}, []
    for name in NAMES:
        a = np.ascontiguousarray(inputs[name])
        arrays[f"in_{name}"] = a
        args.append(nc.dram_tensor(f"in_{name}", a.shape, mybir.dt.from_np(a.dtype), kind="ExternalInput").ap())
    args.append(nc.dram_tensor("out_0", (B, L, C), F32, kind="ExternalOutput").ap())
    args.append(nc.dram_tensor("gates", (B, 2, C), F32, kind="Internal").ap())
    dit_block(nc, *args)
    r = run_bass_kernel_spmd(nc, [arrays], core_ids=[0])
    return r.results[0]["out_0"]
```

```python
from contextlib import ExitStack

import concourse.bass as bass
from concourse import mybir
from concourse.alu_op_type import AluOpType as ALU

F32 = mybir.dt.float32
F32R = mybir.dt.float32r
ACT = mybir.ActivationFunctionType
AX = mybir.AxisListType

B, L, C = 32, 256, 288
H = 16
D = C // H
FF = 4 * C
EPS = 1e-6
P = 128
NT = L // P
REM = C - 2 * P
KR = 3 * REM
CX = C + 2 * REM
KRB = KR + 2
PAIRS = H // 2
QUADS = H // 4
HB = 64
KS = 3 * D
KSM = KS + 1
VB = 32
NF = FF // P
FU = (NF + 1) // 2
FC2_PARTS = 3
NV = 4
SCALE = float(D) ** -0.5

QKV_USES = 2 + 3 * NT
FU_ALT = FU // 2
MLP_USES = 2 + NT + 2 + (FU - FU_ALT) + NT
TURN_USES = 2 * QUADS
USE_PROJ, USE_LT, USE_FC1, USE_FC2 = 2, 2 + NT, 4 + NT, MLP_USES - NT

PE_ORDER = [
    ("t2", -1, 7), ("s", 0, 0), ("t1", 0, 1), ("xt", 1, 0), ("fc2", -2, 0), ("st", -1, 7), ("fc2", -2, 1),
    ("t1", 0, 2), ("fc2", -2, 2), ("s", 0, 1), ("t2", 0, 0), ("pv", -1, 3), ("xt", 1, 1), ("st", 0, 0), ("fc2", -2, 3),
    ("on", -1, 3), ("fc2", -2, 4), ("fc2", -2, 5), ("t2", 0, 1), ("s", 0, 2), ("t1", 0, 3), ("ot", -1, 0),
    ("st", 0, 1), ("s", 0, 3), ("t1", 0, 4), ("ot", -1, 1), ("t2", 0, 2), ("qkv", 1, 0), ("pv", 0, 0), ("st", 0, 2),
    ("proj", -1, 0), ("on", 0, 0), ("qkv", 1, 1), ("t2", 0, 3), ("proj", -1, 1), ("s", 0, 4), ("t1", 0, 5),
    ("st", 0, 3), ("qkv", 1, 2), ("t2", 0, 4), ("pv", 0, 1), ("s", 0, 5), ("t1", 0, 6), ("st", 0, 4), ("on", 0, 1),
    ("lt", -1, 0), ("qkv", 1, 3), ("t2", 0, 5), ("t1", 0, 7), ("lt", -1, 1), ("s", 0, 6), ("st", 0, 5), ("fc1", -1, 0),
    ("fc1", -1, 1), ("t2", 0, 6), ("fc1", -1, 2), ("fc1", -1, 3), ("fc1", -1, 4), ("s", 0, 7), ("st", 0, 6),
    ("qkv", 1, 4), ("t1", 1, 0), ("pv", 0, 2), ("qkv", 1, 5), ("on", 0, 2),
]

ACT_ORDER = [
    ("qkv", 0, 5), ("t1", 0, 1), ("st", -1, 7), ("xt", 1, 0), ("pv", -1, 3), ("t1", 0, 2), ("xt", 1, 1), ("st", 0, 0),
    ("t1", 0, 3), ("ot", -1, 0), ("st", 0, 1), ("t1", 0, 4), ("ot", -1, 1), ("qkv", 1, 0), ("pv", 0, 0), ("st", 0, 2),
    ("qkv", 1, 1), ("t1", 0, 5), ("st", 0, 3), ("qkv", 1, 2), ("pv", 0, 1), ("t1", 0, 6), ("st", 0, 4), ("lt", -1, 0),
    ("t1", 0, 7), ("lt", -1, 1), ("qkv", 1, 3), ("st", 0, 5), ("fc1", -1, 0), ("fc1", -1, 1), ("fc1", -1, 2),
    ("fc1", -1, 3), ("fc1", -1, 4), ("st", 0, 6), ("qkv", 1, 4), ("pv", 0, 2), ("t1", 1, 0),
]

DVE_ORDER = [
    ("max", 0, 0), ("max", 0, 1), ("xt", 1, 0), ("t2", 0, 0), ("sum2", -2, 0), ("max", 0, 2), ("max", 0, 3),
    ("xt", 1, 1), ("on", -1, 3), ("sum2", -2, 1), ("t2", 0, 1), ("max", 0, 4), ("max", 0, 5), ("ot", -1, 0),
    ("max", 0, 6), ("max", 0, 7), ("t2", 0, 2), ("ot", -1, 1), ("qkv", 1, 0), ("proj", -1, 0), ("t2", 0, 3),
    ("on", 0, 0), ("qkv", 1, 1), ("proj", -1, 1), ("max", 0, 8), ("max", 0, 9), ("ln2_stats", -1, 0), ("qkv", 1, 2),
    ("t2", 0, 4), ("ln2_apply", -1, 0), ("ln2_apply", -1, 1), ("max", 0, 10), ("max", 0, 11), ("lt", -1, 0),
    ("on", 0, 1), ("t2", 0, 5), ("lt", -1, 1), ("max", 0, 12), ("qkv", 1, 3), ("max", 0, 13), ("t2", 0, 6),
    ("fc1", -1, 0), ("fc1", -1, 1), ("fc1", -1, 2), ("fc1", -1, 3), ("fc1", -1, 4), ("ln1_stats", 2, 0),
    ("max", 0, 14), ("max", 0, 15), ("ln1_apply", 2, 0), ("ln1_apply", 2, 1), ("t2", 0, 7), ("on", 0, 2),
]

POOL_ORDER = [
    ("xt", 1, 0), ("sum2", -2, 0), ("sum2", -2, 1), ("proj", -1, 0), ("proj", -1, 1), ("ln2_stats", -1, 0),
    ("ln2_apply", -1, 1), ("lt", -1, 0), ("fc1", -1, 0), ("fc1", -1, 1), ("fc1", -1, 2), ("ln1_stats", 2, 0),
    ("fc1", -1, 3), ("fc1", -1, 4),
]

SYNC_ORDER = [
    ("s", 0, 0), ("s", 0, 1), ("s", 0, 2), ("sum2", -2, 1), ("ot", -1, 0), ("s", 0, 3), ("s", 0, 4), ("s", 0, 5),
    ("s", 0, 6), ("ln1_stats", 2, 0), ("s", 0, 7),
]

QKV_ORDER = [(0, 0), (0, 1), (1, 0), (1, 1), (0, 2), (1, 2)]
QK_USES = 2 + 4


class Batch:

    def __init__(self, half, k):
        self.half, self.k = half, k
        self.par = k % 2

    def times(self, n, plus):
        return self.half * (2 * n) + (self.k * n + plus)

    def pairs(self, n, plus):
        return self.half * n + (self.k // 2 * n + plus)

    def looped(self):
        return not isinstance(self.half, int)

    def number(self):
        return self.half * 2 + self.k


def wait(eng, sem, value):
    if not (isinstance(value, int) and value <= 0):
        eng.wait_ge(sem, value)


def run(eng, order, steps):
    def iteration(half, k, only=True):
        for name, off, n in order:
            if only and not 0 <= 2 * half + k + off < B:
                continue
            if name in steps:
                steps[name](Batch(half, k + off), n)

    for k in (-1, 0, 1):
        iteration(0, k)
    with eng.Fori(1, B // 2 - 1) as half:
        for k in (0, 1):
            iteration(half, k, only=False)
    for k in range(B - 2, B + 2):
        iteration(0, k)


def dit_block(nc, x, cond, w_qkv, b_qkv, w_proj, b_proj, w_fc1, b_fc1, w_fc2, b_fc2, w_ada, b_ada, out, gates_dram):
    with ExitStack() as ctx:
        def sb(name, shape, dt=F32):
            return ctx.enter_context(nc.sbuf_tensor(name, shape, dt))

        def sem(name):
            return ctx.enter_context(nc.semaphore(name))

        score_bank = [ctx.enter_context(nc.psum_tensor(f"score_bank{t}", [P, 512], F32)) for t in range(2)]
        st_bank = ctx.enter_context(nc.psum_tensor("st_bank", [P, 2, NT, L], F32))
        t2_ps = st_bank[:, 0, 0, :]
        t1_bank = ctx.enter_context(nc.psum_tensor("t1_bank", [P, 512], F32))
        turn_bank = ctx.enter_context(nc.psum_tensor("turn_bank", [P, 512], F32))
        qkv_bank = ctx.enter_context(nc.psum_tensor("qkv_bank", [P, 512], F32))
        mlp_bank = ctx.enter_context(nc.psum_tensor("mlp_bank", [P, 512], F32))

        wq = sb("wq", [P, 5, 3 * C], F32R)
        wp = sb("wp", [P, 5, C], F32R)
        w1 = sb("w1", [P, 5, FF], F32R)
        w2 = sb("w2", [P, 2, NF, C], F32R)
        ident = sb("ident", [P, P])
        ident_r = sb("ident_r", [P, P], F32R)
        minus_lo = sb("minus_lo", [P, 1])
        mhalf = sb("mhalf", [P, NT])
        mod = sb("mod", [P, NV * 3, B])
        xin = sb("xin", [P, 2, NT, C])
        xn = sb("xn", [P, NT, CX])
        mod1 = sb("mod1", [P, 6])
        stat1 = sb("stat1", [P, NT, 6])
        mv1 = sb("mv1", [P, NT, 2])
        ve1 = sb("ve1", [P, NT])
        rs1 = sb("rs1", [P, NT])
        v1 = sb("v1", [P, 3, L])
        xh1 = sb("xh1", [P, 2, L], F32R)
        xl1 = sb("xl1", [P, 2, L], F32R)
        xr1 = sb("xr1", [P, L], F32R)
        qs = sb("qs", [P, 2, NT, H, HB], F32R)
        ks = sb("ks", [P, 2, NT, H, HB], F32R)
        ve = sb("ve", [P, 2, NT, H, VB])
        qk1 = sb("qk1", [P, 4, 2, L], F32R)
        q2 = sb("q2", [P, 2, L], F32R)
        e = sb("e", [P, 4, 2, NT, L])
        ots = sb("ots", [P, L])
        rc = sb("rc", [P, NT, 4, 1])
        onat = sb("onat", [P, NT, CX])
        gate = sb("gate", [P, 2, 3, C])
        xres = sb("xres", [P, NT, C])
        tmp = sb("tmp", [P, NT, C])
        x1 = sb("x1", [P, NT, C])
        xn2 = sb("xn2", [P, NT, CX])
        mod2 = sb("mod2", [P, 6])
        stat2 = sb("stat2", [P, NT, 6])
        mv2 = sb("mv2", [P, NT, 2])
        ve2 = sb("ve2", [P, NT])
        rs2 = sb("rs2", [P, NT])
        v3 = sb("v3", [P, 3, L])
        xh3 = sb("xh3", [P, 2, L], F32R)
        xl3 = sb("xl3", [P, 2, L], F32R)
        xr3 = sb("xr3", [P, L], F32R)
        g = sb("g", [P, NF * L])
        gh = sb("gh", [P, NF * L], F32R)
        gl = sb("gl", [P, NF * L], F32R)

        consts = sem("consts")
        iota_step = sem("iota_step")
        w_loaded = [sem(f"w_loaded{i}") for i in range(2)]
        w_hi = sem("w_hi")
        wq_hi = sem("wq_hi")
        w_split = sem("w_split")
        c_loaded = sem("c_loaded")
        ada_loaded = sem("ada_loaded")
        ada_exp = sem("ada_exp")
        silu_step = sem("silu_step")
        ada_turned = sem("ada_turned")
        ada_sT = sem("ada_sT")
        ada_mm = sem("ada_mm")
        ada_row = sem("ada_row")
        ada_step = sem("ada_step")
        mod_turned = sem("mod_turned")
        gates_ready = sem("gates_ready")
        mod_ready = sem("mod_ready")
        gates_stored = sem("gates_stored")
        x_loaded = [sem(f"x_loaded{i}") for i in range(2)]
        ln1_dve = sem("ln1_dve")
        rstd1 = sem("rstd1")
        mod1_set = sem("mod1_set")
        qkv_full = sem("qkv_full")
        qkv_drained = sem("qkv_drained")
        alt_full = sem("alt_full")
        alt_drained = sem("alt_drained")
        x1_hi = sem("x1_hi")
        x1_lo = sem("x1_lo")
        x1_rem = sem("x1_rem")
        qk_hi = sem("qk_hi")
        t1_full = sem("t1_full")
        t1_drained = sem("t1_drained")
        s_full = [sem(f"s_full{i}") for i in range(2)]
        s_max = [sem(f"s_max{i}") for i in range(2)]
        t2_full = sem("t2_full")
        q2_ready = sem("q2_ready")
        turn_full = sem("turn_full")
        turn_drained = sem("turn_drained")
        st_full = sem("st_full")
        e_ready = sem("e_ready")
        recip = sem("recip")
        gate_loaded = [sem(f"gate_loaded{i}") for i in range(2)]
        res_loaded = sem("res_loaded")
        mlp_full = sem("mlp_full")
        mlp_drained = sem("mlp_drained")
        o_ready = sem("o_ready")
        o_hi = sem("o_hi")
        summed = sem("summed")
        ln2_dve = sem("ln2_dve")
        biased = sem("biased")
        rstd2 = sem("rstd2")
        mod2_set = sem("mod2_set")
        x3_hi = sem("x3_hi")
        x3_lo = sem("x3_lo")
        x3_rem = sem("x3_rem")
        g_hi = sem("g_hi")
        g_lo = sem("g_lo")
        stored = sem("stored")
        passed = sem("passed")

        stage = [g[:, 0:FF], g[:, FF:2 * FF]]
        NS = len(stage)
        loads = []
        for w, bias, dst, n in ((w_qkv, b_qkv, wq, 3 * C), (w_proj, b_proj, wp, C), (w_fc1, b_fc1, w1, FF)):
            loads += [("full", w, bias, dst, n, 0), ("full", w, bias, dst, n, 1), ("rem", w, bias, dst, n, 0)]
        loads += [("fc2", w_fc2, None, w2, 3 * C, f) for f in range(0, NF, 3)]
        staged, load_count = [0] * NS, []
        for i, load in enumerate(loads):
            staged[i % NS] += 16 * {"full": 1, "rem": 5, "fc2": 1}[load[0]]
            load_count.append(staged[i % NS])

        K_ROWS = [(0, P), (P, P), (2 * P, REM)]
        e_flat = e[:, :, :, :, :].rearrange("p a b c d -> p (a b c d)")
        w_ada_sb = [e_flat[:, 0:6 * C], e_flat[:, 6 * C:12 * C],
                    ve[:, :, :, :, :].rearrange("p a b c d -> p (a b c d)")[0:REM, 0:6 * C]]
        c_in, c_exp = x1[0:B, 0, :], x1[0:B, 1, :]
        c_sig, c_silu = tmp[0:B, 0, :], tmp[0:B, 1, :]
        sT = onat[:, 0, 0:3 * B].rearrange("p (k b) -> p k b", k=3)
        MOD_OF = [0, 1, 3, 4]
        GATE_OF = [2, 5]
        ADA_ORDER = [0, 1, 3, 4, 2, 5]
        ada_bank = [score_bank[0][:, :], score_bank[1][:, :], t1_bank[:, :],
                    st_bank[:, 0, :, :].rearrange("p u l -> p (u l)"), st_bank[:, 1, :, :].rearrange("p u l -> p (u l)"),
                    mlp_bank[:, :]]
        mod_row = {0: onat[0:B, 1, :], 1: e_flat[0:B, 12 * C:12 * C + CX], 3: xn2[0:B, 0, :], 4: xn2[0:B, 1, :]}
        gate_val = gate[0:B, 1, :, :]
        v1_row, v3_row = (v[0:B, :, :].rearrange("b c l -> b (c l)")[:, 0:2 * C] for v in (v1, v3))
        bias_row = {0: v1_row[:, 0:C], 1: v1_row[:, C:2 * C], 3: v3_row[:, 0:C], 4: v3_row[:, C:2 * C],
                    2: xres[0:B, 0, :], 5: xres[0:B, 1, :]}
        b_fc2_row = e_flat[0:B, 12 * C + CX:13 * C + CX]
        MOD_PS = turn_bank[:, 0:NV * 3 * B].rearrange("p (v b) -> p v b", b=B)
        N_ADA = 3 + 5

        def tiles_split_with(b, j):
            i = 3 + PAIRS * b.k + j
            return i if not b.looped() and i < len(loads) else None

        def products(xh, xl, xr, w):
            return [(xh[:, 0, :], w[:, 0, :]), (xh[:, 1, :], w[:, 1, :]), (xh[:, 0, :], w[:, 2, :]),
                    (xh[:, 1, :], w[:, 3, :]), (xl[:, 0, :], w[:, 0, :]), (xl[:, 1, :], w[:, 1, :]),
                    (xr[0:KRB, :], w[0:KRB, 4, :])]

        def fc1_use(b, n, plus=0):
            if n % 2:
                return qkv_bank, alt_full, alt_drained, b.times(FU_ALT, n // 2 + plus)
            return mlp_bank, mlp_full, mlp_drained, b.times(MLP_USES, USE_FC1 + n // 2 + plus)

        block = ctx.enter_context(nc.Block())

        @block.sync
        def _(sp):
            sp.dma_start(c_in, cond).then_inc(c_loaded, 16)
            for k, (r0, nr) in enumerate(K_ROWS):
                sp.dma_start(w_ada_sb[k], w_ada[r0:r0 + nr, :]).then_inc(ada_loaded, 16)
            for to, c0, n in ((v1_row, 0, 2 * C), (v3_row, 3 * C, 2 * C), (bias_row[2], 2 * C, C), (bias_row[5], 5 * C, C)):
                sp.dma_start(to, b_ada[c0:c0 + n].rearrange("(a c) -> a c", a=1).broadcast_to([B, n])
                             ).then_inc(ada_loaded, 16)

            sp.dma_start(b_fc2_row, b_fc2.rearrange("(a c) -> a c", a=1).broadcast_to([B, C])).then_inc(ada_loaded, 16)

            def load_weights(i):
                kind, w, bias, dst, n, k = loads[i]
                if i >= NS:
                    sp.wait_ge(w_split, i - NS + 1)
                s, to = w_loaded[i % NS], stage[i % NS]
                if kind == "full":
                    sp.dma_start(to[:, 0:n], w[k * P:(k + 1) * P, :]).then_inc(s, 16)
                elif kind == "rem":
                    for r in range(3):
                        sp.dma_start(to[REM * r:REM * (r + 1), 0:n], w[2 * P:C, :]).then_inc(s, 16)
                    for r in range(2):
                        sp.dma_start(to[KR + r:KR + r + 1, 0:n], bias.rearrange("(a n) -> a n", a=1)).then_inc(s, 16)
                else:
                    sp.dma_start(to[:, 0:n].rearrange("p (f c) -> p f c", f=3),
                                 w[k * P:(k + 3) * P, :].rearrange("(f p) c -> p f c", p=P)).then_inc(s, 16)

            def row(ap, b):
                return ap[b.k] if isinstance(b.half, int) and b.half == 0 else ap[b.number()]

            def load_x(b, _):
                wait(sp, ln1_dve, b.times(4, -4))
                sp.dma_start(xin[:, b.par], row(x, b).rearrange("(p t) c -> p t c", t=NT)
                             ).then_inc(x_loaded[b.par], 16)

            load_x(Batch(0, 0), 0)
            for i in range(3):
                load_weights(i)

            def load_residual(b, n):
                if n:
                    return
                if not b.looped() and b.k == 0:
                    sp.wait_ge(gates_ready, 3)
                    sp.dma_start(gates_dram, gate_val).then_inc(gates_stored, 16)
                    sp.wait_ge(gates_stored, 16)
                wait(sp, summed, b.times(4, -2))
                sp.dma_start(xres[:, :, :], row(x, b).rearrange("(p t) c -> p t c", t=NT)
                             ).then_inc(res_loaded, 16)
                sp.dma_start(gate[:, b.par], row(gates_dram, b).unsqueeze(0).broadcast_to([P, 3, C])
                             ).then_inc(gate_loaded[b.par], 16)

            def store(b, n):
                if n == NT - 1:
                    sp.wait_ge(summed, b.times(4, 4))
                    sp.dma_start(row(out, b).rearrange("(p t) c -> p t c", t=NT), x1[:, :, :]).then_inc(stored, 16)

            def more_weights(b, j):
                i = tiles_split_with(b, j)
                if i is not None:
                    load_weights(i)

            run(sp, SYNC_ORDER, {"ln1_stats": load_x, "ot": load_residual, "sum2": store, "s": more_weights})
            sp.wait_ge(stored, 16 * B)

        @block.tensor
        def _(pe):
            pe.wait_ge(iota_step, 2)
            pe.wait_ge(silu_step, 3)
            for k, (r0, nr) in enumerate(K_ROWS):
                last = nc.tensor.transpose(t1_bank[0:nr, k * B:(k + 1) * B], c_silu[:, r0:r0 + nr], ident[0:B, 0:B])
            last.then_inc(ada_turned, 1)
            pe.wait_ge(ada_sT, 1)
            pe.wait_ge(ada_loaded, 16 * N_ADA)
            for v in ADA_ORDER:
                if v == ADA_ORDER[-1]:
                    pe.wait_ge(ada_step, NV)
                    for i, m in enumerate(MOD_OF):
                        for tile, width in enumerate((P, P, KR)):
                            last = nc.tensor.transpose(MOD_PS[0:width, 3 * i + tile, :],
                                                       mod_row[m][:, tile * P:tile * P + width], ident[0:B, 0:B])
                    last.then_inc(mod_turned, 1)
                for k, (_r, nr) in enumerate(K_ROWS):
                    last = nc.tensor.matmul(ada_bank[v][0:B, 0:C], sT[0:nr, k, :], w_ada_sb[k][:, v * C:(v + 1) * C],
                                            start=(k == 0), stop=(k == 2))
                last.then_inc(ada_mm, 1)

            def need_weights(b, n):
                if not b.looped() and b.k == 0:
                    pe.wait_ge(w_split, n)

            def turn_x(bank, xn_, n):
                for t in range(NT):
                    if n == 0:
                        for c in range(2):
                            last = nc.tensor.transpose(bank[:, c * L + t * P:c * L + (t + 1) * P],
                                                       xn_[:, t, c * P:(c + 1) * P], ident[:, :])
                    else:
                        last = nc.tensor.transpose(bank[0:KR, t * P:(t + 1) * P], xn_[:, t, 2 * P:CX],
                                                   ident[:, :])
                return last

            def xt(b, n):
                pe.wait_ge(ln1_dve, b.times(4, 4))
                wait(pe, qkv_drained, b.times(QKV_USES, n))
                turn_x(qkv_bank, xn, n).then_inc(qkv_full, 1)

            def qkv(b, n):
                t, w = QKV_ORDER[n]
                need_weights(b, 3)
                pe.wait_ge(x1_lo, b.times(1, 1))
                pe.wait_ge(x1_rem, b.times(1, 1))
                pe.wait_ge(qkv_drained, b.times(QKV_USES, 2 + n))
                if w == 2:
                    wait(pe, alt_drained, b.times(FU_ALT, -FU_ALT))
                pr = products(xh1, xl1, xr1, wq)
                for i, (xa, wa) in enumerate(pr):
                    last = nc.tensor.matmul(qkv_bank[:, 0:C], xa[:, t * P:(t + 1) * P], wa[:, w * C:(w + 1) * C],
                                            start=(i == 0), stop=(i == len(pr) - 1))
                last.then_inc(qkv_full, 1)

            def t1(b, j):
                if j == 0:
                    pe.wait_ge(qkv_drained, b.times(QKV_USES, QK_USES))
                    if not b.looped() and b.k == 0:
                        pe.wait_ge(consts, 3)
                        pe.wait_ge(gates_ready, 3)
                        pe.wait_ge(mod_ready, 1)
                wait(pe, t1_drained, b.times(PAIRS, j))
                for i, src in enumerate((qs, ks)):
                    for t in range(NT):
                        last = nc.tensor.transpose(t1_bank[:, i * L + t * P:i * L + (t + 1) * P].bitcast(F32R),
                                                   src[:, b.par, t, 2 * j:2 * j + 2, :], ident_r[:, :])
                last.then_inc(t1_full, 1)

            def s(b, j):
                pe.wait_ge(t1_drained, b.times(PAIRS, j + 1))
                for i in range(2):
                    wait(pe, s_max[i], b.times(PAIRS, j))
                    rows = slice(HB * i, HB * i + KS)
                    for t in range(NT):
                        last = nc.tensor.matmul(score_bank[i][:, t * L:(t + 1) * L],
                                                qk1[rows, j % 4, 0, t * P:(t + 1) * P], qk1[rows, j % 4, 1, :],
                                                start=True, stop=True)
                    last.then_inc(s_full[i], 1)

            def t2(b, j):
                for i in range(2):
                    pe.wait_ge(s_max[i], b.times(PAIRS, j + 1))
                wait(pe, e_ready, b.times(PAIRS, j))
                for t in range(NT):
                    last = nc.tensor.transpose(t2_ps[:, t * P:(t + 1) * P].bitcast(F32R),
                                               qs[:, b.par, t, 2 * j:2 * j + 2, :], ident_r[:, :])
                last.then_inc(t2_full, 1)

            def st(b, j):
                pe.wait_ge(q2_ready, b.times(PAIRS, j + 1))
                for i in range(2):
                    rows = slice(HB * i, HB * i + KSM)
                    for u in range(NT):
                        last = nc.tensor.matmul(st_bank[:, i, u, :], qk1[rows, j % 4, 1, u * P:(u + 1) * P],
                                                q2[rows, j % 2, :], start=True, stop=True)
                last.then_inc(st_full, 1)

            def pv(b, q):
                pe.wait_ge(e_ready, b.times(PAIRS, 2 * q + 2))
                if q == 0:
                    pe.wait_ge(qkv_drained, b.times(QKV_USES, QKV_USES))
                wait(pe, turn_drained, b.times(TURN_USES, 2 * q))
                for u in range(NT):
                    for c in range(4):
                        last = nc.tensor.matmul(turn_bank[VB * c:VB * (c + 1), 0:L], ve[:, b.par, u, 4 * q + c, :],
                                                e[:, 2 * (q % 2) + c // 2, c % 2, u, :],
                                                start=(u == 0), stop=(u == NT - 1))
                last.then_inc(turn_full, 1)

            def on(b, q):
                pe.wait_ge(turn_drained, b.times(TURN_USES, 2 * q + 1))
                for t in range(NT):
                    last = nc.tensor.transpose(turn_bank[:, t * P:(t + 1) * P], ots[:, t * P:(t + 1) * P], ident[:, :])
                last.then_inc(turn_full, 1)

            def ot(b, n):
                pe.wait_ge(o_ready, b.times(1, 1))
                wait(pe, mlp_drained, b.times(MLP_USES, n))
                turn_x(mlp_bank, onat, n).then_inc(mlp_full, 1)

            def proj(b, t):
                need_weights(b, 6)
                pe.wait_ge(mlp_drained, b.times(MLP_USES, USE_PROJ + t))
                pr = products(xh3, xl3, xr3, wp)
                for i, (xa, wa) in enumerate(pr):
                    last = nc.tensor.matmul(mlp_bank[:, 0:C], xa[:, t * P:(t + 1) * P], wa,
                                            start=(i == 0), stop=(i == len(pr) - 1))
                last.then_inc(mlp_full, 1)

            def lt(b, n):
                pe.wait_ge(ln2_dve, b.times(4, 4))
                pe.wait_ge(mlp_drained, b.times(MLP_USES, USE_LT + n))
                turn_x(mlp_bank, xn2, n).then_inc(mlp_full, 1)

            def fc1(b, n):
                pe.wait_ge(x3_lo, b.times(1, 1))
                pe.wait_ge(x3_rem, b.times(1, 1))
                need_weights(b, 9)
                bank, full, drained, use = fc1_use(b, n)
                wait(pe, drained, use)
                if n % 2:
                    qk_done = b.times(QKV_USES, 2 * QKV_USES + QK_USES)
                    pe.wait_ge(qkv_drained, qk_done if b.looped() else min(qk_done, B * QKV_USES))
                for f in range(2 * n, min(2 * n + 2, NF)):
                    pr = products(xh3, xl3, xr3, w1)
                    for i, (xa, wa) in enumerate(pr):
                        last = nc.tensor.matmul(bank[:, (f % 2) * L:(f % 2 + 1) * L], wa[:, f * P:(f + 1) * P], xa,
                                                start=(i == 0), stop=(i == len(pr) - 1))
                last.then_inc(full, 1)

            def fc2(b, n):
                t, part = n // FC2_PARTS, n % FC2_PARTS
                if part == 0:
                    need_weights(b, len(loads))
                    pe.wait_ge(g_lo, b.times(FU, FU))
                    pe.wait_ge(mlp_drained, b.times(MLP_USES, USE_FC2 + t))
                for f in range(part * NF // FC2_PARTS, (part + 1) * NF // FC2_PARTS):
                    cols = slice(f * L + t * P, f * L + (t + 1) * P)
                    nc.tensor.matmul(mlp_bank[:, 0:C], gh[:, cols], w2[:, 0, f, :], start=(f == 0), stop=False)
                    nc.tensor.matmul(mlp_bank[:, 0:C], gh[:, cols], w2[:, 1, f, :], start=False, stop=False)
                    last = nc.tensor.matmul(mlp_bank[:, 0:C], gl[:, cols], w2[:, 0, f, :], start=False,
                                            stop=(f == NF - 1))
                if part == FC2_PARTS - 1:
                    last.then_inc(mlp_full, 1)

            run(pe, PE_ORDER, {"xt": xt, "qkv": qkv, "t1": t1, "s": s, "t2": t2, "st": st, "pv": pv, "on": on, "ot": ot,
                     "proj": proj, "lt": lt, "fc1": fc1, "fc2": fc2})

        @block.scalar
        def _(act):
            act.wait_ge(c_loaded, 16)
            nc.scalar.activation(c_exp, c_in, ACT.Exp, scale=-1.0).then_inc(ada_exp, 1)
            for i in range(3):
                kind, _w, _bias, dst, n, k = loads[i]
                act.wait_ge(w_loaded[i % NS], load_count[i])
                if kind == "full":
                    nc.scalar.copy(dst[:, k, :], stage[i % NS][:, 0:n]).then_inc(wq_hi, 1)
                else:
                    nc.scalar.copy(dst[0:KRB, 4, :], stage[i % NS][0:KRB, 0:n]).then_inc(wq_hi, 1)

            def xt(b, n):
                pe_use = b.times(QKV_USES, n + 1)
                act.wait_ge(mod1_set, b.times(1, 1))
                if n == 0:
                    wait(act, x1_lo, b.times(1, 0))
                    wait(act, x1_rem, b.times(1, 0))
                act.wait_ge(qkv_full, pe_use)
                for c in (0, 1) if n == 0 else (2,):
                    rows = P if c < 2 else KR
                    last = nc.scalar.activation(v1[0:rows, c, :], qkv_bank[0:rows, (c % 2) * L:(c % 2 + 1) * L],
                                                ACT.Identity, bias=mod1[0:rows, c:c + 1], scale=mod1[0:rows, 3 + c:4 + c])
                last.then_inc(qkv_drained, 1)

            def qkv(b, n):
                t, w = QKV_ORDER[n]
                act.wait_ge(qkv_full, b.times(QKV_USES, 3 + n))
                src = qkv_bank[:, 0:C].rearrange("p (h d) -> p h d", h=H)
                if w == 2:
                    nc.scalar.copy(ve[:, b.par, t, :, 0:D], src).then_inc(qkv_drained, 1)
                else:
                    to = (qs[:, b.par, t, :, 0:2 * D], ks[:, b.par, t, :, D:KS])[w]
                    nc.scalar.copy(to.rearrange("p h (r d) -> p h r d", r=2),
                                   src.unsqueeze(2).broadcast_to([P, H, 2, D])).then_inc(qk_hi, 1)

            def t1(b, j):
                act.wait_ge(t1_full, b.times(PAIRS, j + 1))
                nc.scalar.copy(qk1[:, j % 4, :, :].rearrange("p i l -> p (i l)"), t1_bank[:, :]).then_inc(t1_drained, 1)

            def st(b, j):
                act.wait_ge(st_full, b.times(PAIRS, j + 1))
                nc.scalar.activation(e[:, j % 4, :, :, :].rearrange("p i u l -> p (i u l)"),
                                     st_bank[:, :, :, :].rearrange("p i u l -> p (i u l)"),
                                     ACT.Exp, scale=SCALE).then_inc(e_ready, 1)

            def pv(b, q):
                act.wait_ge(turn_full, b.times(TURN_USES, 2 * q + 1))
                nc.scalar.copy(ots[:, :], turn_bank[:, 0:L]).then_inc(turn_drained, 1)

            def ot(b, n):
                act.wait_ge(mlp_full, b.times(MLP_USES, n + 1))
                if n == 0:
                    nc.scalar.copy(xh3[:, :, :].rearrange("p c l -> p (c l)"), mlp_bank[:, :]).then_inc(o_hi, 1)
                else:
                    nc.scalar.copy(xr3[0:KR, :], mlp_bank[0:KR, 0:L]).then_inc(o_hi, 1)

            def lt(b, n):
                act.wait_ge(mod2_set, b.times(1, 1))
                if n == 0:
                    wait(act, x3_lo, b.times(1, 0))
                    wait(act, x3_rem, b.times(1, 0))
                act.wait_ge(mlp_full, b.times(MLP_USES, USE_LT + n + 1))
                for c in (0, 1) if n == 0 else (2,):
                    rows = P if c < 2 else KR
                    last = nc.scalar.activation(v3[0:rows, c, :], mlp_bank[0:rows, (c % 2) * L:(c % 2 + 1) * L],
                                                ACT.Identity, bias=mod2[0:rows, c:c + 1], scale=mod2[0:rows, 3 + c:4 + c])
                last.then_inc(mlp_drained, 1)

            def fc1(b, n):
                wait(act, g_lo, b.times(FU, n + 1 - FU))
                if not b.looped() and b.k == 0:
                    act.wait_ge(w_split, len(loads))
                bank, full, drained, count = fc1_use(b, n, 1)
                act.wait_ge(full, count)
                cols = min(2 * L, NF * L - 2 * L * n)
                nc.scalar.activation(g[:, 2 * L * n:2 * L * n + cols], bank[:, 0:cols], ACT.Gelu_apprx_tanh
                                     ).then_inc(drained, 1)

            run(act, ACT_ORDER, {"xt": xt, "qkv": qkv, "t1": t1, "st": st, "pv": pv, "ot": ot, "lt": lt, "fc1": fc1})

        @block.vector
        def _(dve):
            nc.vector.memset(mod[:, :, :], 0.0)
            nc.vector.memset(minus_lo[:, :], 0.0).then_inc(w_hi, 1)
            dve.wait_ge(w_hi, 1)
            nc.vector.memset(minus_lo[REM:2 * REM, 0:1], -1.0)
            nc.vector.memset(minus_lo[KR:P, 0:1], -1.0).then_inc(w_hi, 1)
            dve.wait_ge(w_hi, 2)
            nc.vector.memset(minus_lo[KR:KR + 1, 0:1], 0.0)
            nc.vector.memset(mhalf[:, :], -0.5)
            nc.vector.memset(xr1[KR:KRB, :].bitcast(F32), 1.0)
            nc.vector.memset(xr3[KR:KRB, :].bitcast(F32), 1.0)
            dve.wait_ge(iota_step, 2)
            nc.vector.tensor_copy(ident_r[:, :], ident[:, :])
            dve.wait_ge(c_loaded, 16)
            dve.wait_ge(ada_exp, 1)
            nc.vector.tensor_scalar(c_exp, c_exp, 1.0, None, ALU.add).then_inc(silu_step, 1)
            dve.wait_ge(silu_step, 1)
            nc.vector.reciprocal(c_sig, c_exp).then_inc(silu_step, 1)
            dve.wait_ge(silu_step, 2)
            nc.vector.tensor_tensor(c_silu, c_in, c_sig, ALU.mult).then_inc(silu_step, 1)
            dve.wait_ge(ada_turned, 1)
            nc.vector.tensor_copy(sT[:, 0:2, :], t1_bank[:, 0:2 * B].rearrange("p (k b) -> p k b", k=2))
            nc.vector.tensor_copy(sT[0:REM, 2, :], t1_bank[0:REM, 2 * B:3 * B]).then_inc(ada_sT, 1)
            nc.vector.memset(ks[:, :, :, :, KSM:HB].bitcast(F32), 0.0)
            nc.vector.memset(ks[:, :, :, :, KS:KSM].bitcast(F32), -1.0).then_inc(consts, 1)
            def split_weights(i, hi_by_act=False):
                kind, w, bias, dst, n, k = loads[i]
                dve.wait_ge(w_loaded[i % NS], load_count[i])
                if hi_by_act:
                    dve.wait_ge(wq_hi, i + 1)
                src = stage[i % NS][:, 0:n]
                if kind in ("full", "fc2"):
                    if kind == "full":
                        hi, lo = dst[:, k, :], dst[:, 2 + k, :]
                    else:
                        hi, lo = (dst[:, i_, k:k + 3, :].rearrange("p f c -> p (f c)") for i_ in range(2))
                    if not hi_by_act:
                        nc.vector.tensor_copy(hi, src).then_inc(w_hi, 1)
                        dve.wait_ge(w_hi, i)
                    nc.vector.tensor_tensor(lo, src, hi.bitcast(F32), ALU.subtract).then_inc(w_split, 1)
                else:
                    to, m, src = dst[0:KRB, 4, :], minus_lo[0:KRB, 0:1], src[0:KRB]
                    if not hi_by_act:
                        nc.vector.tensor_copy(to, src).then_inc(w_hi, 1)
                        dve.wait_ge(w_hi, i)
                    nc.vector.scalar_tensor_tensor(to, to.bitcast(F32), m, src, ALU.mult, ALU.add).then_inc(w_split, 1)

            def statistics(src, stat, mv, var_eps, steps, b, ready):
                for t in range(NT):
                    ready(t)
                    last = nc.vector.bn_stats(stat[:, t, :], src[:, t, :])
                last.then_inc(steps, 1)
                dve.wait_ge(steps, b.times(4, 1))
                dve.sem_inc(passed, 1)
                for t in range(NT):
                    last = nc.vector.bn_aggr(mv[:, t, :], stat[:, t, :])
                last.then_inc(steps, 1)
                dve.wait_ge(steps, b.times(4, 2))
                nc.vector.tensor_scalar(var_eps[:, :], mv[:, :, 1], EPS, None, ALU.add).then_inc(steps, 1)

            def normalise(src, mv, rs, dst, steps, rstd, b, t):
                dve.wait_ge(rstd, b.times(1, 1))
                nc.vector.tensor_scalar(dst[:, t, 0:C], src[:, t, :], mv[:, t, 0:1], rs[:, t:t + 1],
                                        ALU.subtract, ALU.mult)
                last = nc.vector.tensor_scalar(dst[:, t, C:CX].rearrange("p (r c) -> p r c", r=2),
                                               src[:, t, 2 * P:C].unsqueeze(1).broadcast_to([P, 2, REM]),
                                               mv[:, t, 0:1], rs[:, t:t + 1], ALU.subtract, ALU.mult)
                if t == NT - 1:
                    last.then_inc(steps, 1)

            def ln1_stats(b, _):
                statistics(xin[:, b.par], stat1, mv1, ve1, ln1_dve, b,
                           lambda t: dve.wait_ge(x_loaded[b.par], b.pairs(16, 16)) if t == 0 else None)

            def ln1_apply(b, t):
                normalise(xin[:, b.par], mv1, rs1, xn, ln1_dve, rstd1, b, t)

            dve.wait_ge(ada_loaded, 16 * N_ADA)
            for i, v in enumerate(ADA_ORDER):
                dve.wait_ge(ada_mm, i + 1)
                if v in GATE_OF:
                    nc.vector.tensor_tensor(gate_val[:, v // 3, :], ada_bank[v][0:B, 0:C], bias_row[v], ALU.add
                                            ).then_inc(gates_ready, 1)
                else:
                    nc.vector.scalar_tensor_tensor(mod_row[v][:, 0:C], ada_bank[v][0:B, 0:C], float(v % 3), bias_row[v],
                                                   ALU.add, ALU.add).then_inc(ada_row, 1)
                    dve.wait_ge(ada_row, i + 1)
                    nc.vector.tensor_copy(mod_row[v][:, C:CX].rearrange("b (r c) -> b r c", r=2),
                                          mod_row[v][:, 2 * P:C].unsqueeze(1).broadcast_to([B, 2, REM])
                                          ).then_inc(ada_step, 1)
                if i == 0:
                    ln1_stats(Batch(0, 0), 0)
                elif i in (1, 2):
                    split_weights(i - 1, True)
                elif i == 3:
                    for t in range(NT):
                        ln1_apply(Batch(0, 0), t)
                elif i == 4:
                    dve.wait_ge(mod_turned, 1)
                    mod4 = mod[:, :, :].rearrange("p (v c) b -> p v c b", c=3)
                    ps4 = MOD_PS.rearrange("p (v c) b -> p v c b", c=3)
                    nc.vector.tensor_copy(mod4[:, :, 0:2, :], ps4[:, :, 0:2, :])
                    nc.vector.tensor_copy(mod4[0:KR, :, 2, :], ps4[0:KR, :, 2, :]).then_inc(mod_ready, 1)
            dve.wait_ge(gates_ready, 2)
            nc.vector.tensor_tensor(gate_val[:, 2, :], gate_val[:, 1, :], b_fc2_row, ALU.mult).then_inc(gates_ready, 1)
            split_weights(2, True)

            def remainder(v, xr, hi, rem, b):
                nc.vector.tensor_copy(xr[0:KR, :], v[0:KR, 2, :]).then_inc(hi, 1)
                dve.wait_ge(hi, b.times(2, 2))
                low = xr[2 * REM:KR, :]
                nc.vector.tensor_tensor(low, v[2 * REM:KR, 2, :], low.bitcast(F32), ALU.subtract).then_inc(rem, 1)

            def xt(b, n):
                dve.wait_ge(qkv_drained, b.times(QKV_USES, n + 1))
                if n == 0:
                    nc.vector.tensor_copy(xh1[:, :, :], v1[:, 0:2, :]).then_inc(x1_hi, 1)
                else:
                    remainder(v1, xr1, x1_hi, x1_rem, b)

            def qkv(b, n):
                t, w = QKV_ORDER[n]
                if w == 2:
                    return
                dve.wait_ge(qk_hi, b.times(2 * NT, 2 * t + w + 1))
                tile = (qs, ks)[w][:, b.par, t]
                hi, lo = (tile[:, :, 0:D], tile[:, :, 2 * D:KS]) if w == 0 else (tile[:, :, D:2 * D], tile[:, :, 0:D])
                nc.vector.tensor_tensor(lo, qkv_bank[:, 0:C].rearrange("p (h d) -> p h d", h=H), hi.bitcast(F32),
                                        ALU.subtract).then_inc(qkv_drained, 1)

            def head_max(b, h):
                j, i = h // 2, h % 2
                dve.wait_ge(s_full[i], b.times(PAIRS, j + 1))
                nc.vector.tensor_reduce(qs[:, b.par, :, h, KS:KSM],
                                        score_bank[i][:, :].rearrange("p (t l) -> p t l", t=NT),
                                        AX.X, ALU.max).then_inc(s_max[i], 1)
                tile = tiles_split_with(b, j)
                if i == 1 and tile is not None:
                    split_weights(tile)

            def t2(b, j):
                dve.wait_ge(t2_full, b.times(PAIRS, j + 1))
                nc.vector.tensor_copy(q2[:, j % 2, :], t2_ps).then_inc(q2_ready, 1)

            def on(b, q):
                dve.wait_ge(turn_full, b.times(TURN_USES, 2 * q + 1 + 1))
                o = turn_bank[:, 0:NT * P].rearrange("p (t c v) -> p t c v", t=NT, c=4)
                nc.vector.reciprocal(rc[:, :, :, :], o[:, :, :, D:D + 1]).then_inc(recip, 1)
                dve.wait_ge(recip, b.times(QUADS, q + 1))
                to = onat[:, :, 4 * D * q:4 * D * (q + 1)].rearrange("p t (c d) -> p t c d", c=4)
                nc.vector.tensor_tensor(to, o[:, :, :, 0:D], rc[:, :, :, :].broadcast_to([P, NT, 4, D]), ALU.mult
                                        ).then_inc(turn_drained, 1)
                if q == QUADS - 1:
                    dve.wait_ge(turn_drained, b.times(TURN_USES, TURN_USES))
                    for t in range(NT):
                        last = nc.vector.tensor_copy(onat[:, t, C:CX].rearrange("p (r c) -> p r c", r=2),
                                                     onat[:, t, 2 * P:C].unsqueeze(1).broadcast_to([P, 2, REM]))
                    last.then_inc(o_ready, 1)

            def ot(b, n):
                dve.wait_ge(o_hi, b.times(2, n + 1))
                if n == 0:
                    nc.vector.tensor_tensor(xl3[:, :, :].rearrange("p c l -> p (c l)"), mlp_bank[:, :],
                                            xh3[:, :, :].rearrange("p c l -> p (c l)").bitcast(F32), ALU.subtract
                                            ).then_inc(mlp_drained, 1)
                else:
                    low = xr3[2 * REM:KR, :]
                    nc.vector.tensor_tensor(low, mlp_bank[2 * REM:KR, 0:L], low.bitcast(F32), ALU.subtract
                                            ).then_inc(mlp_drained, 1)

            def gated(b, t, use, which):
                wait(dve, summed, b.times(4, 2 * which + t - 1))
                dve.wait_ge(mlp_full, b.times(MLP_USES, use + t + 1))
                nc.vector.tensor_tensor(tmp[:, t, :], mlp_bank[:, 0:C], gate[:, b.par, which, :], ALU.mult
                                        ).then_inc(mlp_drained, 1)

            def proj(b, t):
                dve.wait_ge(gate_loaded[b.par], b.pairs(16, 16))
                gated(b, t, USE_PROJ, 0)

            def ln2_stats(b, _):
                statistics(x1, stat2, mv2, ve2, ln2_dve, b, lambda t: dve.wait_ge(summed, b.times(4, 1 + t)))

            def ln2_apply(b, t):
                normalise(x1, mv2, rs2, xn2, ln2_dve, rstd2, b, t)

            def lt(b, n):
                dve.wait_ge(mlp_drained, b.times(MLP_USES, USE_LT + n + 1))
                if n == 0:
                    nc.vector.tensor_copy(xh3[:, :, :], v3[:, 0:2, :]).then_inc(x3_hi, 1)
                else:
                    remainder(v3, xr3, x3_hi, x3_rem, b)

            def fc1(b, n):
                _bank, _full, drained, count = fc1_use(b, n, 1)
                dve.wait_ge(drained, count)
                cols = slice(2 * L * n, min(2 * L * (n + 1), NF * L))
                nc.vector.tensor_copy(gh[:, cols], g[:, cols]).then_inc(g_hi, 1)

            def sum2(b, t):
                gated(b, t, USE_FC2, 1)

            run(dve, DVE_ORDER, {"ln1_stats": ln1_stats, "ln1_apply": ln1_apply, "xt": xt, "qkv": qkv, "max": head_max, "t2": t2, "on": on,
                      "ot": ot, "proj": proj, "ln2_stats": ln2_stats, "ln2_apply": ln2_apply, "lt": lt, "fc1": fc1,
                      "sum2": sum2})

        @block.gpsimd
        def _(pool):
            nc.gpsimd.memset(ident[:, :], 0.0).then_inc(iota_step, 1)
            pool.wait_ge(iota_step, 1)
            nc.gpsimd.affine_select(out=ident[:, :], in_=ident[:, :], compare_op=ALU.not_equal, fill=1.0, base=0,
                                    pattern=[[-1, P]], channel_multiplier=1).then_inc(iota_step, 1)
            nc.gpsimd.memset(qs[:, :, :, :, KS:HB].bitcast(F32), 0.0).then_inc(consts, 1)

            def ln1_vectors(b):
                wait(pool, qkv_drained, b.times(QKV_USES, 2 - QKV_USES))
                nc.gpsimd.tensor_copy(mod1[:, :], column(0, b)).then_inc(mod1_set, 1)

            def ln1_power(b):
                pool.wait_ge(ln1_dve, b.times(4, 3))
                nc.gpsimd.tensor_tensor(rs1[:, :], ve1[:, :], mhalf[:, :], ALU.pow).then_inc(rstd1, 1)

            def ln1(b, _):
                ln1_vectors(b)
                ln1_power(b)

            def ln2(b, _):
                wait(pool, mlp_drained, b.times(MLP_USES, USE_LT + 2 - MLP_USES))
                nc.gpsimd.tensor_copy(mod2[:, :], column(6, b)).then_inc(mod2_set, 1)
                pool.wait_ge(ln2_dve, b.times(4, 3))
                nc.gpsimd.tensor_tensor(rs2[:, :], ve2[:, :], mhalf[:, :], ALU.pow).then_inc(rstd2, 1)

            def column(v0, b):
                k = b.k if isinstance(b.half, int) else b.number()
                return mod[:, v0:v0 + 6, k:k + 1] if isinstance(k, int) else mod[:, v0:v0 + 6, bass.ds(k, 1)]

            ln1_power(Batch(0, 0))
            pool.wait_ge(mod_ready, 1)
            ln1_vectors(Batch(0, 0))
            pool.wait_ge(ada_mm, 6)
            nc.gpsimd.memset(ve[:, :, :, :, D:VB], 1.0).then_inc(consts, 1)

            def xt(b, n):
                if n == 0:
                    pool.wait_ge(x1_hi, b.times(2, 1))
                    nc.gpsimd.tensor_tensor(xl1[:, :, :], v1[:, 0:2, :], xh1[:, :, :].bitcast(F32), ALU.subtract
                                            ).then_inc(x1_lo, 1)

            def lt(b, n):
                if n == 0:
                    pool.wait_ge(x3_hi, b.times(2, 1))
                    nc.gpsimd.tensor_tensor(xl3[:, :, :], v3[:, 0:2, :], xh3[:, :, :].bitcast(F32), ALU.subtract
                                            ).then_inc(x3_lo, 1)

            def proj(b, t):
                pool.wait_ge(res_loaded, b.times(16, 16))
                wait(pool, stored, b.times(16, 0))
                pool.wait_ge(mlp_drained, b.times(MLP_USES, USE_PROJ + t + 1))
                nc.gpsimd.tensor_tensor(x1[:, t, :], tmp[:, t, :], xres[:, t, :], ALU.add).then_inc(summed, 1)

            def fc1(b, n):
                pool.wait_ge(g_hi, b.times(FU, n + 1))
                cols = slice(2 * L * n, min(2 * L * (n + 1), NF * L))
                nc.gpsimd.tensor_tensor(gl[:, cols], g[:, cols], gh[:, cols].bitcast(F32), ALU.subtract
                                        ).then_inc(g_lo, 1)

            def fc2_bias(b, t):
                if t == NT - 1:
                    pool.wait_ge(ln2_dve, b.times(4, 4))
                    nc.gpsimd.tensor_tensor(x1[:, :, :], x1[:, :, :], gate[:, b.par, 2:3, :].broadcast_to([P, NT, C]),
                                            ALU.add).then_inc(biased, 1)

            def sum2(b, t):
                pool.wait_ge(biased, b.times(1, 1))
                pool.wait_ge(mlp_drained, b.times(MLP_USES, USE_FC2 + t + 1))
                nc.gpsimd.tensor_tensor(x1[:, t, :], tmp[:, t, :], x1[:, t, :], ALU.add).then_inc(summed, 1)

            run(pool, POOL_ORDER, {"ln1_stats": ln1, "ln2_stats": ln2, "xt": xt, "lt": lt, "proj": proj, "ln2_apply": fc2_bias, "fc1": fc1,
                       "sum2": sum2})


NAMES = ["x", "cond_1152", "L0_cond_W_qkv", "L0_cond_b_qkv", "L0_cond_W_proj", "L0_cond_b_proj", "L0_cond_W_fc1",
         "L0_cond_b_fc1", "L0_cond_W_fc2", "L0_cond_b_fc2", "L0_cond_W_ada", "L0_cond_b_ada"]


def kernel(**inputs):
    import numpy as np
    from concourse import bacc
    from concourse.bass_utils import run_bass_kernel_spmd

    nc = bacc.Bacc("TRN2", target_bir_lowering=False, num_devices=1)
    arrays, args = {}, []
    for name in NAMES:
        a = np.ascontiguousarray(inputs[name])
        arrays[f"in_{name}"] = a
        args.append(nc.dram_tensor(f"in_{name}", a.shape, mybir.dt.from_np(a.dtype), kind="ExternalInput").ap())
    args.append(nc.dram_tensor("out_0", (B, L, C), F32, kind="ExternalOutput").ap())
    args.append(nc.dram_tensor("gates", (B, 3, C), F32, kind="Internal").ap())
    dit_block(nc, *args)
    r = run_bass_kernel_spmd(nc, [arrays], core_ids=[0])
    return r.results[0]["out_0"]
```
